# Optimizing a Trainium2 kernel written in Bass

```python
import numpy as np
import jax
import jax.numpy as jnp

def _softmax(x, axis=-1):
    return jax.nn.softmax(x, axis=axis)

def _gelu(x):
    return jax.nn.gelu(x, approximate=True)

def _silu(x):
    return jax.nn.silu(x)

def _sigmoid(x):
    return jax.nn.sigmoid(x)

def _layernorm(x, axis=-1, eps=1e-05):
    m = jnp.mean(x, axis=axis, keepdims=True)
    v = jnp.var(x, axis=axis, keepdims=True)
    return (x - m) / jnp.sqrt(v + eps)

def _scatter_add(tgt, idx, src, axis=0):
    return tgt.at[idx].add(src)

def _segment_sum(src, seg, n):
    return jax.ops.segment_sum(src, seg, n)
kernel_name = 'mk_gnn_preln_d2_gnn_r8_f8fe67'

def setup_inputs(seed: int=0):
    np.random.seed(seed)
    _w = jnp.asarray

    def _rec_inputs():
        import jax
        import jax.numpy as jnp
        _gk = jax.random.key(seed)
        x = -0.0003713 + 1 * jax.random.normal(jax.random.fold_in(_gk, 1), (6250, 256), jnp.float32)
        src = jax.random.randint(jax.random.fold_in(_gk, 2), (100000,), 0, 6250, jnp.int32)
        dst = jax.random.randint(jax.random.fold_in(_gk, 3), (100000,), 0, 6250, jnp.int32)
        _o = jnp.argsort(dst, stable=True)
        src = src[_o]
        dst = dst[_o]
        edge_type_2 = jax.random.randint(jax.random.fold_in(_gk, 13), (100000,), 0, 2, jnp.int32)
        return (x, src, dst, edge_type_2)
    x, src, dst, edge_type_2 = _rec_inputs()

    def _L0_gnn_setup():
        import jax, jax.numpy as jnp
        import numpy as np
        N, E, D, L = (6250, 200000, 256, 3)
        EPS = 1e-05
        key = jax.random.key(seed)
        ks = jax.random.split(key, 10)
        x = jax.random.normal(ks[0], (N, D), dtype=jnp.float32)
        edge_index = jax.random.randint(ks[1], (2, E), 0, N, dtype=jnp.int32)
        mask_embed = jax.random.normal(ks[2], (D,), dtype=jnp.float32)
        s = 1.0 / np.sqrt(D)
        Wl = jax.random.normal(ks[3], (L, D, D), dtype=jnp.float32) * s
        Wr = jax.random.normal(ks[4], (L, D, D), dtype=jnp.float32) * s
        b = jax.random.normal(ks[5], (L, D), dtype=jnp.float32) * 0.01
        gamma = 1.0 + 0.1 * jax.random.normal(ks[6], (L, D), dtype=jnp.float32)
        beta = 0.1 * jax.random.normal(ks[7], (L, D), dtype=jnp.float32)
        rmean = 0.1 * jax.random.normal(ks[8], (L, D), dtype=jnp.float32)
        rvar = 0.5 + jax.random.uniform(ks[9], (L, D), dtype=jnp.float32)
        return {'x': x, 'edge_index': edge_index, 'mask_embed': mask_embed, 'Wl': Wl, 'Wr': Wr, 'b': b, 'gamma': gamma, 'beta': beta, 'rmean': rmean, 'rvar': rvar}
    _L0_gnn_all = _L0_gnn_setup()
    _L0_gnn_in = {k: v for k, v in _L0_gnn_all.items() if k in ('mask_embed', 'Wl', 'Wr', 'b', 'gamma', 'beta', 'rmean', 'rvar')}
    del _L0_gnn_all

    def _L1_gnn_setup():
        import jax, jax.numpy as jnp
        import numpy as np
        N_NODES = 1250
        N_EDGES = 40000
        D = 256
        D_OUT = 256
        NUM_REL = 2
        key = jax.random.key(seed)
        ks = jax.random.split(key, 16)
        s = 1.0 / np.sqrt(D)
        inp = {}
        inp['feat'] = jax.random.normal(ks[0], (N_NODES, D), dtype=jnp.float32)
        inp['src'] = jax.random.randint(ks[1], (N_EDGES,), 0, N_NODES, dtype=jnp.int32)
        inp['dst'] = jax.random.randint(ks[2], (N_EDGES,), 0, N_NODES, dtype=jnp.int32)
        inp['rel'] = jax.random.randint(ks[3], (N_EDGES,), 0, NUM_REL, dtype=jnp.int32)
        inp['W_rel'] = jax.random.normal(ks[4], (NUM_REL, D, D), dtype=jnp.float32) * s
        inp['b_rel'] = jax.random.normal(ks[5], (NUM_REL, D), dtype=jnp.float32) * s
        inp['W_ih'] = jax.random.normal(ks[6], (4 * D, D), dtype=jnp.float32) * s
        inp['b_ih'] = jax.random.normal(ks[7], (4 * D,), dtype=jnp.float32) * s
        inp['b_hh'] = jax.random.normal(ks[8], (4 * D,), dtype=jnp.float32) * s
        h = D // 2
        inp['W1'] = jax.random.normal(ks[9], (h, D), dtype=jnp.float32) * s
        inp['b1'] = jax.random.normal(ks[10], (h,), dtype=jnp.float32) * s
        inp['W2'] = jax.random.normal(ks[11], (h, h), dtype=jnp.float32) * (1.0 / np.sqrt(h))
        inp['b2'] = jax.random.normal(ks[12], (h,), dtype=jnp.float32) * (1.0 / np.sqrt(h))
        inp['W3'] = jax.random.normal(ks[13], (D_OUT, h), dtype=jnp.float32) * (1.0 / np.sqrt(h))
        inp['b3'] = jax.random.normal(ks[14], (D_OUT,), dtype=jnp.float32) * (1.0 / np.sqrt(h))
        return inp
    _L1_gnn_all = _L1_gnn_setup()
    _L1_gnn_in = {k: v for k, v in _L1_gnn_all.items() if k in ('W_rel', 'b_rel', 'W_ih', 'b_ih', 'b_hh', 'W1', 'b1', 'W2', 'b2', 'W3', 'b3')}
    del _L1_gnn_all
    return {'x': x, 'src': src, 'dst': dst, 'edge_type_2': edge_type_2, 'L0_gnn_mask_embed': _L0_gnn_in['mask_embed'], 'L0_gnn_Wl': _L0_gnn_in['Wl'], 'L0_gnn_Wr': _L0_gnn_in['Wr'], 'L0_gnn_b': _L0_gnn_in['b'], 'L0_gnn_gamma': _L0_gnn_in['gamma'], 'L0_gnn_beta': _L0_gnn_in['beta'], 'L0_gnn_rmean': _L0_gnn_in['rmean'], 'L0_gnn_rvar': _L0_gnn_in['rvar'], 'L1_gnn_W_rel': _L1_gnn_in['W_rel'], 'L1_gnn_b_rel': _L1_gnn_in['b_rel'], 'L1_gnn_W_ih': _L1_gnn_in['W_ih'], 'L1_gnn_b_ih': _L1_gnn_in['b_ih'], 'L1_gnn_b_hh': _L1_gnn_in['b_hh'], 'L1_gnn_W1': _L1_gnn_in['W1'], 'L1_gnn_b1': _L1_gnn_in['b1'], 'L1_gnn_W2': _L1_gnn_in['W2'], 'L1_gnn_b2': _L1_gnn_in['b2'], 'L1_gnn_W3': _L1_gnn_in['W3'], 'L1_gnn_b3': _L1_gnn_in['b3']}

def reference(x, src, dst, edge_type_2, L0_gnn_mask_embed, L0_gnn_Wl, L0_gnn_Wr, L0_gnn_b, L0_gnn_gamma, L0_gnn_beta, L0_gnn_rmean, L0_gnn_rvar, L1_gnn_W_rel, L1_gnn_b_rel, L1_gnn_W_ih, L1_gnn_b_ih, L1_gnn_b_hh, L1_gnn_W1, L1_gnn_b1, L1_gnn_W2, L1_gnn_b2, L1_gnn_W3, L1_gnn_b3):
    import jax
    import jax.numpy as jnp

    def _L0_gnn_ref(x, edge_index, mask_embed, Wl, Wr, b, gamma, beta, rmean, rvar):
        import jax, jax.numpy as jnp
        import numpy as np
        N, E, D, L = (6250, 200000, 256, 3)
        EPS = 1e-05
        src, dst = (edge_index[0], edge_index[1])
        h = x.at[0].set(mask_embed)
        deg = jax.ops.segment_sum(jnp.ones((src.shape[0],), h.dtype), dst, num_segments=N)
        deg = jnp.maximum(deg, 1.0)[:, None]
        for i in range(L):
            agg = jax.ops.segment_sum(h[src], dst, num_segments=N) / deg
            z = agg @ Wl[i] + b[i] + h @ Wr[i]
            z = (z - rmean[i]) * jax.lax.rsqrt(rvar[i] + EPS) * gamma[i] + beta[i]
            if i != L - 1:
                z = jax.nn.relu(z)
            z = z + h
            h = z
        return h

    def _L1_gnn_ref(feat, src, dst, rel, W_rel, b_rel, W_ih, b_ih, b_hh, W1, b1, W2, b2, W3, b3):
        import jax, jax.numpy as jnp
        import numpy as np
        N_NODES = 1250
        N_EDGES = 40000
        D = 256
        D_OUT = 256
        NUM_REL = 2
        n_nodes = feat.shape[0]
        S = feat[src]

        def edge_nn(x, W, b):
            h = jax.nn.relu(x @ W.T + b)
            return jax.nn.relu(h @ W.T + b)
        msgs = jnp.zeros_like(S)
        for r in range(W_rel.shape[0]):
            msgs = jnp.where((rel == r)[:, None], edge_nn(S, W_rel[r], b_rel[r]), msgs)
        agg = jax.ops.segment_sum(msgs, dst, num_segments=n_nodes)
        gates = agg @ W_ih.T + b_ih + b_hh
        i, f, g, o = jnp.split(gates, 4, axis=-1)
        c = jax.nn.sigmoid(i) * jnp.tanh(g)
        hn = jax.nn.sigmoid(o) * jnp.tanh(c)
        x = jax.nn.relu(hn @ W1.T + b1)
        x = jax.nn.relu(x @ W2.T + b2)
        return x @ W3.T + b3
    edge_index = jnp.stack([src, dst])
    h = jnp.maximum(_layernorm(x, axis=-1), 0.0)
    x = x + _L0_gnn_ref(h, edge_index, L0_gnn_mask_embed, L0_gnn_Wl, L0_gnn_Wr, L0_gnn_b, L0_gnn_gamma, L0_gnn_beta, L0_gnn_rmean, L0_gnn_rvar)
    h = jnp.maximum(_layernorm(x, axis=-1), 0.0)
    x = x + _L1_gnn_ref(h, src, dst, edge_type_2, L1_gnn_W_rel, L1_gnn_b_rel, L1_gnn_W_ih, L1_gnn_b_ih, L1_gnn_b_hh, L1_gnn_W1, L1_gnn_b1, L1_gnn_W2, L1_gnn_b2, L1_gnn_W3, L1_gnn_b3)
    return x

_drawn_inputs = setup_inputs


def setup_inputs(seed=0):
    import zlib

    import numpy as np

    out = dict(_drawn_inputs(seed))
    spreads = {}
    factors = {'L0_gnn_mask_embed': 6.633,
     'L0_gnn_b': 8.0,
     'L1_gnn_b_rel': 6.422,
     'L1_gnn_b_ih': 64.0,
     'L1_gnn_b_hh': 59.666,
     'L1_gnn_b1': 6.005,
     'L1_gnn_b2': 3.718}
    for name, (base, spread) in spreads.items():
        noise = np.random.default_rng([zlib.crc32(name.encode()), seed]).standard_normal(out[name].shape)
        drawn = base * np.exp(spread * noise) if base else spread * noise
        out[name] = jnp.asarray(drawn.astype(out[name].dtype))
    for name, factor in factors.items():
        out[name] = (out[name] * factor).astype(out[name].dtype)
    return out
```

```python
from contextlib import ExitStack

import concourse.bass as bass
from concourse import mybir

F32 = mybir.dt.float32
I32 = mybir.dt.int32
ALU = mybir.AluOpType
ACT = mybir.ActivationFunctionType

N, E, D = 6250, 100000, 256
P = 128
KD = D // P
TN = 125
TILES = N // TN
EP, EC = 125, E // 125
GROUP = 16
HALF = GROUP // 2
CHUNKS = -(-(E // P + TILES) // GROUP) * GROUP
GROUPS = CHUNKS // GROUP
BLOCKS = -(-CHUNKS // P)
CP = BLOCKS * P
LEAD = GROUPS - TILES
W = D + 1
CROW = CP // 2
PS = 4
LAYERS = 3
EPS = 1e-5
SRC_BITS = 13
DST_SHIFT, REL_SHIFT = SRC_BITS, 2 * SRC_BITS
BIG = float(1 << 20)
XB = 5
assert TN * TILES == N and EP * EC == E and CHUNKS * P >= E + TILES * P and LEAD >= 1
HOOKS = {0: (3, 6), 2: (2, 4, 8, 10, 13), 3: (2, 4, 8, 10, 12)}


def gnn(nc, x, src, dst, rel, mask_embed, Wl, Wr, b, gamma, beta, rmean, rvar,
        WrelT, b_rel, WihT, b_ih, b_hh, W1T, b1, W2T, b2, W3T, b3, out):
    ctx = ExitStack()
    with ctx:
        ctx.enter_context(nc.allow_non_contiguous_dma(reason="bias columns and row ends: a few elements"))

        def sb(name, shape, dt=F32):
            return ctx.enter_context(nc.sbuf_tensor(name, shape, dt))

        def sem(name):
            return ctx.enter_context(nc.semaphore(name))

        rec_dram = nc.dram_tensor("rec_dram", (E + P,), I32, kind="Internal").ap()
        slot_dram = nc.dram_tensor("slot_dram", (CP * P,), I32, kind="Internal").ap()
        H = [nc.dram_tensor(f"h{i}_dram", (N, D), F32, kind="Internal").ap() for i in range(LAYERS)]
        X1 = nc.dram_tensor("x1_dram", (N, D), F32, kind="Internal").ap()
        MSG = nc.dram_tensor("msg_dram", (2 * N, D), F32, kind="Internal").ap()

        ident = sb("ident", [P, P])
        ones = sb("ones", [P, P])
        tri = sb("tri", [P, P])
        node_iota = sb("node_iota", [P, TN])
        slot_iota = sb("slot_iota", [P, P])
        chunk_iota = sb("chunk_iota", [TILES, CP])
        chunk_start = sb("chunk_start", [P, BLOCKS])
        bound = sb("bound", [P, TILES + 1])
        tile_p = sb("tile_p", [TILES, 4])
        eps_col = sb("eps_col", [P, 1])
        wl = sb("wl", [P, LAYERS, KD, D])
        wr = sb("wr", [P, LAYERS, KD, D])
        bn = sb("bn", [P, 2, LAYERS * D])
        bnrow = sb("bnrow", [1, 3, LAYERS * D])
        wrel = sb("wrel", [P, 2, KD, D])
        brelc = sb("brelc", [P, 2, KD])
        brelr = sb("brelr", [1, 2, D])
        wih = sb("wih", [P, KD, 4 * D])
        bihc = sb("bihc", [P, 2, 8])
        w1 = sb("w1", [P, KD, P])
        w2 = sb("w2", [P, P])
        w3 = sb("w3", [P, D])
        b12 = sb("b12", [P, 2])
        b3r = sb("b3r", [1, D])
        idx0 = sb("idx0", [P, CP], I32)
        idx1 = sb("idx1", [P, CP], I32)
        dloc = sb("dloc", [P, CP])
        keep = sb("keep", [P, CP])
        toff = sb("toff", [1, CP], I32)
        flags = sb("flags", [1, 2], I32)
        acc = sb("acc", [P, TILES * W])
        rows = sb("rows", [P, GROUP, W])
        onehot = sb("onehot", [P, GROUP, TN])
        idx_st = sb("idx_st", [P, GROUP], I32)
        deg = sb("deg", [P, 2])
        aggn = sb("aggn", [P, D])
        ht = sb("ht", [P, D])
        xt = sb("xt", [P, D])
        tT = sb("tT", [P, 4, TN])
        hn = sb("hn", [P, D])
        x1t = sb("x1t", [P, D])
        stat = sb("stat", [P, 12])
        y1 = sb("y1", [P, 4, TN])
        msg = sb("msg", [P, 2, D])
        gate = sb("gate", [P, 6, TN])
        cell = sb("cell", [P, 2, 2, TN])
        z12 = sb("z12", [P, 2, TN])

        e_dst = sb("e_dst", [EP, EC], I32)
        e_src = sb("e_src", [EP, EC], I32)
        e_rel = sb("e_rel", [EP, EC], I32)
        e_rec = sb("e_rec", [EP, EC], I32)
        e_f = sb("e_f", [EP, EC])
        e_next = sb("e_next", [EP, 1], I32)
        e_nextf = sb("e_nextf", [EP, 1])
        bad = sb("bad", [EP, 3])
        cntb = sb("cntb", [EP, TILES + 1])
        zero_i = sb("zero_i", [P, P], I32)
        tl = sb("tl", [TILES, 8])
        tli = sb("tli", [TILES, 1], I32)
        vals = sb("vals", [TILES, 3])
        info = sb("info", [P, BLOCKS, 3])
        run_start = sb("run_start", [P, BLOCKS], I32)
        flagf = sb("flagf", [1, 3])
        blk = sb("blk", [P, BLOCKS, P], I32)
        xs = sb("xs", [TN, 2, XB, D])
        lns = sb("lns", [TN, XB, 6])
        lnm = sb("lnm", [TN, 2, XB, 3])
        e_tmp = sb("e_tmp", [EP, EC])
        st_pos = sb("st_pos", [EP, 8], I32)
        st_rec = sb("st_rec", [EP, 8], I32)
        ncnt = sb("ncnt", [EP, TILES])
        diag = sb("diag", [TILES, TILES])
        slot0 = sb("slot0", [EP, TILES])
        belong = acc[0:TILES, 0:CP]
        first = acc[0:TILES, CP:2 * CP]
        u_rel = acc[:, 2 * CP:3 * CP].bitcast(I32)
        u_f = acc[:, 3 * CP:6 * CP].rearrange("p (k c) -> p k c", k=3)
        e_scan = u_f[0:EP, 0, 0:EC]
        pos_f = u_f[0:EP, 1, 0:EC]
        pos_i = u_f[0:EP, 2, 0:EC].bitcast(I32)
        hot_i = onehot[:, :, :].rearrange("p a b -> p (a b)").bitcast(I32)
        u_src = hot_i[:, 0:CP]
        u_dst = hot_i[:, CP:2 * CP]

        weights = []
        lay = "l (k p) n -> p l k n"
        weights.append((bn[:, 0, :], rvar.rearrange("l d -> (l d)").partition_broadcast(P)))
        weights.append((bn[:, 1, :], gamma.rearrange("l d -> (l d)").partition_broadcast(P)))
        for k, w in enumerate((b, rmean, beta)):
            weights.append((bnrow[0:1, k, :], w.rearrange("(a l) d -> a (l d)", a=1)))
        weights.append((wl[:, :, :, :], Wl.rearrange(lay, p=P)))
        weights.append((wr[:, :, :, :], Wr.rearrange(lay, p=P)))
        weights.append((wrel[:, :, :, :], WrelT.rearrange(lay, p=P)))
        weights.append((brelc[:, :, :], b_rel.rearrange("r (k p) -> p r k", p=P)))
        weights.append((brelr[:, :, :], b_rel.rearrange("(a r) d -> a r d", a=1)))
        weights.append((wih[:, :, :], WihT.rearrange("(k p) n -> p k n", p=P)))
        weights.append((bihc[:, 0, :], b_ih.rearrange("(c p) -> p c", p=P)))
        weights.append((bihc[:, 1, :], b_hh.rearrange("(c p) -> p c", p=P)))
        weights.append((w1[:, :, :], W1T.rearrange("(k p) n -> p k n", p=P)))
        weights.append((w2[:, :], W2T))
        weights.append((w3[:, :], W3T))
        weights.append((b12[:, 0:1], b1.rearrange("(p a) -> p a", a=1)))
        weights.append((b12[:, 1:2], b2.rearrange("(p a) -> p a", a=1)))
        weights.append((b3r[0:1, :], b3.rearrange("(a d) -> a d", a=1)))
        N_WTS = len(weights)
        N_CONST = 16

        def bank(name):
            return ctx.enter_context(nc.psum_tensor(name, [P, 512], F32))

        ps = [bank(f"ps{i}") for i in range(PS)]
        pA, pB, pC, pD = bank("pA"), bank("pB"), bank("pC"), bank("pD")

        s_const = sem("s_const")
        s_wts = sem("s_wts")
        s_edges = sem("s_edges")
        s_float = sem("s_float")
        s_rec = sem("s_rec")
        s_rec_out = sem("s_rec_out")
        s_dv = sem("s_dv")
        s_pe = sem("s_pe")
        s_blk = sem("s_blk")
        s_flags = sem("s_flags")
        s_fill = sem("s_fill")
        s_posr = sem("s_posr")
        s_stage = sem("s_stage")
        s_scat = sem("s_scat")
        s_scat_all = sem("s_scat_all")
        s_pos = sem("s_pos")
        s_run = sem("s_run")
        s_chunks = sem("s_chunks")
        s_scan = sem("s_scan")
        s_scan_pe = sem("s_scan_pe")
        s_unp = sem("s_unp")
        s_turn = sem("s_turn")
        s_x = [sem("s_x0"), sem("s_x1")]
        s_lnstat = sem("s_lnstat")
        s_lnsq = sem("s_lnsq")
        s_lnr = sem("s_lnr")
        s_lnh = sem("s_lnh")
        s_h0 = [sem("s_h00"), sem("s_h01")]
        s_mask = sem("s_mask")
        s_bn = sem("s_bn")
        s_bnsq = sem("s_bnsq")
        s_table = sem("s_table")
        s_held_v = sem("s_held_v")
        s_held_s = sem("s_held_s")
        s_held_g = sem("s_held_g")
        s_idx = sem("s_idx")
        s_rows = [sem(f"s_rows{u}") for u in range(GROUP)]
        s_hot = sem("s_hot")
        s_sum = sem("s_sum")
        s_acc0 = sem("s_acc0")
        s_acc = sem("s_acc")

        def dense_sems(n):
            names = ("loaded", "xloaded", "deg", "res", "scaled", "tr", "trc", "z", "new", "stored", "stored2",
                     "var", "sd", "rstd", "norm", "trh", "trhc", "y1", "y1c", "y2", "y2c",
                     "gates", "gatec", "cell", "cellt", "hid", "w1", "w1c", "w2", "w2c")
            return {k: sem(f"s_{n}_{k}") for k in names}

        S_IN = dense_sems("in")
        S_LATE = dense_sems("late")

        block = ctx.enter_context(nc.Block())

        BASE = {L: L * TILES for L in range(LAYERS + 1)}

        def sp_dense(sp, L, t, S):
            rw = bass.ds(t * TN, TN)
            n = BASE[L]
            if L < LAYERS:
                sp.dma_start(ht[0:TN, :], H[L][rw, :]).then_inc(S["loaded"], 16)
            else:
                sp.dma_start(xt[0:TN, :], X1[rw, :]).then_inc(S["loaded"], 16)
            if L == LAYERS - 1:
                sp.dma_start(xt[0:TN, :], x[rw, :]).then_inc(S["xloaded"], 16)
            if L < LAYERS - 1:
                sp.wait_ge(S["new"], t + (n + 1))
                sp.dma_start(H[L + 1][rw, :], hn[0:TN, :]).then_inc(S["stored"], 16)
                sp.wait_ge(S["stored"], t * 16 + 16 * (n + 1))
            elif L == LAYERS - 1:
                sp.wait_ge(S["new"], t + (n + 1))
                sp.dma_start(X1[rw, :], x1t[0:TN, :]).then_inc(S["stored"], 16)
                sp.wait_ge(S["y2c"], t + 1)
                sp.wait_ge(S["stored"], t * 16 + 16 * (n + 1))
                sp.dma_start(MSG.rearrange("(r n) d -> n r d", r=2)[rw, :, :], msg[0:TN, :, :])\
                    .then_inc(S["stored2"], 16)
                sp.wait_ge(S["stored2"], t * 16 + 16)
            else:
                sp.wait_ge(S["new"], t + (n + 1))
                sp.dma_start(out[rw, :], hn[0:TN, :]).then_inc(S["stored"], 16)
                sp.wait_ge(S["stored"], t * 16 + 16 * (n + 1))

        def dve_scale(v, L, t, S):
            n = BASE[L]
            a = acc[0:TN, bass.ds(t * W, D)]
            if L < LAYERS:
                v.tensor_scalar(deg[0:TN, 0:1], acc[0:TN, bass.ds(t * W + D, 1)], 1.0, None, ALU.max)\
                    .then_inc(S["deg"], 1)
                v.wait_ge(S["deg"], t * 2 + (2 * n + 1))
                v.reciprocal(deg[0:TN, 1:2], deg[0:TN, 0:1]).then_inc(S["deg"], 1)
                v.wait_ge(S["deg"], t * 2 + (2 * n + 2))
                v.tensor_scalar(aggn[0:TN, :], a, deg[0:TN, 1:2], None, ALU.mult)\
                    .then_inc(S["scaled"], 1)
            else:
                v.tensor_copy(aggn[0:TN, :], a).then_inc(S["scaled"], 1)

        def dve_new(v, L, t, S):
            n = BASE[L]
            v.wait_ge(S["z"], t + (n + 1))
            v.wait_ge(S["loaded"], t * 16 + 16 * (n + 1))
            if L < LAYERS - 1:
                v.scalar_tensor_tensor(hn[0:TN, :], pB[0:TN, 0:D], 0.0, ht[0:TN, :], ALU.max, ALU.add)\
                    .then_inc(S["new"], 1)
            elif L == LAYERS - 1:
                v.tensor_tensor(x1t[0:TN, :], pB[0:TN, 0:D], ht[0:TN, :], ALU.add)\
                    .then_inc(S["res"], 1)
                v.wait_ge(S["res"], t + 1)
                v.wait_ge(S["xloaded"], t * 16 + 16)
                v.tensor_tensor(x1t[0:TN, :], x1t[0:TN, :], xt[0:TN, :], ALU.add)\
                    .then_inc(S["new"], 1)
                v.wait_ge(S["new"], t + (n + 1))
                v.bn_stats(stat[0:TN, 0:6], x1t[0:TN, :]).then_inc(S["var"], 1)
                v.wait_ge(S["var"], t * 2 + 1)
                v.sem_inc(s_held_v, 1)
                v.bn_aggr(stat[0:TN, 6:8], stat[0:TN, 0:6]).then_inc(S["var"], 1)
            else:
                v.tensor_tensor(hn[0:TN, :], pB[0:TN, 0:D], xt[0:TN, :], ALU.add)\
                    .then_inc(S["new"], 1)

        def dve_norm(v, t, S):
            v.wait_ge(S["sd"], t + 1)
            v.reciprocal(stat[0:TN, 9:10], stat[0:TN, 8:9]).then_inc(S["rstd"], 1)
            v.wait_ge(S["rstd"], t + 1)
            v.tensor_scalar(hn[0:TN, :], x1t[0:TN, :], stat[0:TN, 6:7], stat[0:TN, 9:10],
                            ALU.subtract, ALU.mult).then_inc(S["norm"], 1)

        def dve_cell(v, t, S):
            v.wait_ge(S["gatec"], t + 1)
            v.tensor_tensor(cell[:, 0, :, :], gate[:, 0:2, :], gate[:, 2:4, :], ALU.mult)\
                .then_inc(S["cell"], 1)
            v.wait_ge(S["cellt"], t + 1)
            v.tensor_tensor(cell[:, 0, :, :], gate[:, 4:6, :], cell[:, 1, :, :], ALU.mult)\
                .then_inc(S["hid"], 1)

        def act_turned(a, L, t, S):
            a.wait_ge(S["tr"], t + (BASE[L] + 1))
            k = 4 if L < LAYERS else 2
            a.copy(tT[:, 0:k, :], pA[:, 0:k * TN].rearrange("p (k n) -> p k n", k=k)).then_inc(S["trc"], 1)

        def act_sd(a, t, S):
            a.wait_ge(S["var"], t * 2 + 2)
            a.activation(stat[0:TN, 8:9], stat[0:TN, 7:8], ACT.Sqrt, bias=eps_col[0:TN, :])\
                .then_inc(S["sd"], 1)

        def act_turned_h(a, t, S):
            a.wait_ge(S["trh"], t + 1)
            a.activation(tT[:, 0:2, :], pA[:, 0:2 * TN].rearrange("p (k n) -> p k n", k=2), ACT.Relu)\
                .then_inc(S["trhc"], 1)

        def act_y1(a, t, S):
            a.wait_ge(S["y1"], t + 1)
            for q in range(4):
                i = a.activation(y1[:, q, :], pC[:, q * TN:(q + 1) * TN], ACT.Relu,
                                 bias=brelc[:, q // 2, q % 2:q % 2 + 1])
            i.then_inc(S["y1c"], 1)

        def act_y2(a, t, S):
            a.wait_ge(S["y2"], t + 1)
            a.activation(msg[0:TN, :, :], pD[0:TN, :].rearrange("p (r d) -> p r d", r=2), ACT.Relu)\
                .then_inc(S["y2c"], 1)

        def act_gates(a, t, S):
            a.wait_ge(S["gates"], t + 1)
            for q, (c, f) in enumerate(((0, ACT.Sigmoid), (1, ACT.Sigmoid), (4, ACT.Tanh),
                                        (5, ACT.Tanh), (6, ACT.Sigmoid), (7, ACT.Sigmoid))):
                p = pB[:, q * TN:(q + 1) * TN] if q < 4 else pC[:, (q - 4) * TN:(q - 3) * TN]
                i = a.activation(gate[:, q, :], p, f, bias=bihc[:, 0, c:c + 1])
            i.then_inc(S["gatec"], 1)
            a.wait_ge(S["cell"], t + 1)
            a.activation(cell[:, 1, :, :], cell[:, 0, :, :], ACT.Tanh).then_inc(S["cellt"], 1)

        def act_mlp(a, t, S, k):
            a.wait_ge(S[f"w{k}"], t + 1)
            a.activation(z12[:, k - 1, :], pD[:, (k - 1) * P:(k - 1) * P + TN], ACT.Relu,
                         bias=b12[:, k - 1:k]).then_inc(S[f"w{k}c"], 1)

        def pe_turn(pe, L, t, S):
            n = BASE[L]
            pe.wait_ge(S["scaled"], t + (n + 1))
            if L < LAYERS:
                pe.wait_ge(S["loaded"], t * 16 + 16 * (n + 1))
            for k in range(4 if L < LAYERS else 2):
                frm = aggn if k < 2 else ht
                i = pe.transpose(pA[:, k * TN:(k + 1) * TN], frm[0:TN, (k % 2) * P:(k % 2 + 1) * P],
                                 ident[0:TN, 0:TN])
            i.then_inc(S["tr"], 1)

        def pe_z(pe, L, t, S):
            pe.wait_ge(S["trc"], t + (BASE[L] + 1))
            for k in range(4):
                w = (wl if k < 2 else wr)[:, L, k % 2, :]
                pe.matmul(pB[0:TN, 0:D], tT[:, k, :], w, start=(k == 0), stop=False)
            pe.matmul(pB[0:TN, 0:D], ones[0:1, 0:TN], bnrow[0:1, 0, L * D:(L + 1) * D],
                      start=False, stop=True).then_inc(S["z"], 1)

        def pe_turn_h(pe, t, S):
            pe.wait_ge(S["norm"], t + 1)
            for k in range(2):
                i = pe.transpose(pA[:, k * TN:(k + 1) * TN], hn[0:TN, k * P:(k + 1) * P], ident[0:TN, 0:TN])
            i.then_inc(S["trh"], 1)

        def pe_y1(pe, t, S):
            pe.wait_ge(S["trhc"], t + 1)
            for q in range(4):
                r, m = q // 2, q % 2
                for k in range(2):
                    i = pe.matmul(pC[:, q * TN:(q + 1) * TN], wrel[:, r, k, m * P:(m + 1) * P],
                                  tT[:, k, :], start=(k == 0), stop=(k == 1))
            i.then_inc(S["y1"], 1)

        def pe_y2(pe, t, S):
            pe.wait_ge(S["y1c"], t + 1)
            for r in range(2):
                o = pD[0:TN, r * D:(r + 1) * D]
                for k in range(2):
                    pe.matmul(o, y1[:, 2 * r + k, :], wrel[:, r, k, :], start=(k == 0), stop=False)
                i = pe.matmul(o, ones[0:1, 0:TN], brelr[0:1, r, :], start=False, stop=True)
            i.then_inc(S["y2"], 1)

        def pe_gates(pe, t, S):
            pe.wait_ge(S["trc"], t + (BASE[LAYERS] + 1))
            for q, c in enumerate((0, 1, 4, 5, 6, 7)):
                o = pB[:, q * TN:(q + 1) * TN] if q < 4 else pC[:, (q - 4) * TN:(q - 3) * TN]
                for k in range(2):
                    i = pe.matmul(o, wih[:, k, c * P:(c + 1) * P], tT[:, k, :],
                                  start=(k == 0), stop=(k == 1))
            i.then_inc(S["gates"], 1)

        def pe_w1(pe, t, S):
            pe.wait_ge(S["hid"], t + 1)
            for k in range(2):
                i = pe.matmul(pD[:, 0:TN], w1[:, k, :], cell[:, 0, k, :], start=(k == 0), stop=(k == 1))
            i.then_inc(S["w1"], 1)

        def pe_w2(pe, t, S):
            pe.wait_ge(S["w1c"], t + 1)
            pe.matmul(pD[:, P:P + TN], w2[:, :], z12[:, 0, :], start=True, stop=True).then_inc(S["w2"], 1)

        def pe_w3(pe, t, S):
            pe.wait_ge(S["w2c"], t + 1)
            pe.matmul(pB[0:TN, 0:D], z12[:, 1, :], w3[:, :], start=True, stop=False)
            pe.matmul(pB[0:TN, 0:D], ones[0:1, 0:TN], b3r[0:1, :], start=False, stop=True)\
                .then_inc(S["z"], 1)

        def pe_stages(pe, L, t, S):
            if L < LAYERS - 1:
                return [lambda: pe_turn(pe, L, t, S), lambda: pe_z(pe, L, t, S)]
            if L == LAYERS - 1:
                return [lambda: pe_turn(pe, L, t, S), lambda: pe_z(pe, L, t, S),
                        lambda: pe_turn_h(pe, t, S), lambda: pe_y1(pe, t, S), lambda: pe_y2(pe, t, S)]
            return [lambda: pe_turn(pe, L, t, S), lambda: pe_gates(pe, t, S),
                    lambda: pe_w1(pe, t, S), lambda: pe_w2(pe, t, S), lambda: pe_w3(pe, t, S)]

        def hooks(L):
            return HOOKS[0 if L < LAYERS - 1 else L]

        @block.sync
        def _(sp):
            sp.dma_start(e_dst[:, :], dst.rearrange("(p c) -> p c", c=EC)).then_inc(s_edges, 16)
            sp.dma_start(e_next[0:EP - 1, :], dst.rearrange("(p c) -> p c", c=EC)[1:EP, 0:1])\
                .then_inc(s_edges, 16)
            sp.dma_start(e_src[:, :], src.rearrange("(p c) -> p c", c=EC)).then_inc(s_edges, 16)
            sp.dma_start(e_rel[:, :], rel.rearrange("(p c) -> p c", c=EC)).then_inc(s_edges, 16)
            xv = x.rearrange("(q t p) d -> q p t d", p=TN, t=XB)
            hv = H[0].rearrange("(q t p) d -> q p t d", p=TN, t=XB)
            for q in range(TILES // XB):
                if q >= 2:
                    sp.wait_ge(s_h0[q % 2], 16 * (q // 2))
                sp.dma_start(xs[:, q % 2, :, :], xv[q, :, :, :]).then_inc(s_x[q % 2], 16)
                if q >= 1:
                    sp.wait_ge(s_lnh, q)
                    sp.dma_start(hv[q - 1, :, :, :], xs[:, (q - 1) % 2, :, :])\
                        .then_inc(s_h0[(q - 1) % 2], 16)
            q = TILES // XB
            sp.wait_ge(s_lnh, q)
            sp.dma_start(hv[q - 1, :, :, :], xs[:, (q - 1) % 2, :, :]).then_inc(s_h0[(q - 1) % 2], 16)
            for k in range(2):
                sp.wait_ge(s_h0[k], 16 * (q // 2))
            sp.dma_start(H[0][0:1, :], mask_embed.rearrange("(a d) -> a d", a=1)).then_inc(s_mask, 16)
            sp.wait_ge(s_mask, 16)
            sp.wait_ge(s_rec, 1)
            sp.dma_start(rec_dram[0:E].rearrange("(p c) -> p c", c=EC), e_rec[:, :]).then_inc(s_rec_out, 16)
            sp.dma_start(rec_dram[E:E + P].rearrange("(a d) -> a d", a=1), zero_i[0:1, :])\
                .then_inc(s_rec_out, 16)
            sp.wait_ge(s_rec_out, 32)
            sp.wait_ge(s_flags, 1)
            unsorted = sp.value_load(flags[0:1, 0:1], min_val=0, max_val=1)
            late = sp.value_load(flags[0:1, 1:2], min_val=0, max_val=1)
            with sp.If(unsorted > 0):
                sv = slot_dram.rearrange("(j p c) -> j p c", p=P, c=P)
                for j in range(BLOCKS):
                    sp.dma_start(sv[j, :, :], zero_i[:, :]).then_inc(s_fill, 16)
                sp.wait_ge(s_fill, 16 * BLOCKS)
                sp.wait_ge(s_scat_all, 1)
                sp.dma_start(blk[:, :, :], slot_dram.rearrange("(j p c) -> p j c", p=P, c=P))\
                    .then_inc(s_blk, 16)
                sp.wait_ge(s_blk, 16)
            for L in range(LAYERS + 1):
                with sp.Fori(0, TILES) as t:
                    sp_dense(sp, L, t, S_IN)
                    sp.sem_inc(s_held_s, 1)
                with sp.If(late > 0):
                    with sp.Fori(0, TILES) as t:
                        sp_dense(sp, L, t, S_LATE)
                        sp.sem_inc(s_held_s, 1)

        @block.gpsimd
        def _(g):
            g.memset(ones[:, :], 1.0).then_inc(s_const, 1)
            g.memset(ident[:, :], 0.0).then_inc(s_const, 1)
            g.memset(eps_col[:, :], EPS).then_inc(s_const, 1)
            g.memset(zero_i[:, :], 0).then_inc(s_const, 1)
            g.memset(tile_p[:, 3:4], 0.0).then_inc(s_const, 1)
            g.wait_ge(s_const, 5)
            g.affine_select(out=ident[:, :], in_=ident[:, :], compare_op=ALU.not_equal, fill=1.0, base=0,
                            pattern=[[-1, P]], channel_multiplier=1).then_inc(s_const, 1)
            g.affine_select(out=tri[:, :], in_=ones[:, :], compare_op=ALU.is_gt, fill=0.0, base=0,
                            pattern=[[1, P]], channel_multiplier=-1).then_inc(s_const, 1)
            g.affine_select(out=tile_p[:, 3:4], in_=tile_p[:, 3:4], compare_op=ALU.not_equal, fill=BIG,
                            base=-(TILES - 1), pattern=[[0, 1]], channel_multiplier=1).then_inc(s_const, 1)

            def iota(ap, pattern, base, cm):
                g.iota(ap, pattern=pattern, base=base, channel_multiplier=cm,
                       allow_small_or_imprecise_dtypes=True).then_inc(s_const, 1)

            iota(bound[:, :], [[TN, TILES + 1]], 0, 0)
            iota(node_iota[:, :], [[1, TN]], 0, 0)
            iota(slot_iota[:, :], [[1, P]], 0, 0)
            iota(chunk_iota[:, :], [[1, CP]], 0, 0)
            iota(chunk_start[:, :], [[P * P, BLOCKS]], 0, P)
            iota(tile_p[:, 0:1], [[0, 1]], 0, TN)
            iota(tile_p[:, 1:2], [[0, 1]], 0, W)
            iota(tile_p[:, 2:3], [[0, 1]], GROUP * LEAD, GROUP)
            g.memset(rows[:, :, :], 1.0).then_inc(s_sum, GROUP)
            g.wait_ge(s_flags, 1)
            unsorted = g.value_load(flags[0:1, 0:1], min_val=0, max_val=1)
            late = g.value_load(flags[0:1, 1:2], min_val=0, max_val=1)
            with g.If(unsorted > 0):
                g.wait_ge(s_fill, 16 * BLOCKS)
                with g.Fori(0, EC // 8) as c:
                    g.wait_ge(s_stage, c * 2 + 2)
                    g.sem_inc(s_held_g, 1)
                    for k in range(8):
                        g.indirect_dma_start(
                            slot_dram.rearrange("(n a) -> n a", a=1),
                            bass.IndirectOffsetOnAxis(st_pos[:, k:k + 1], 0),
                            st_rec[:, k:k + 1], None).then_inc(s_scat, 16)
                    g.wait_ge(s_scat, c * 128 + 128)
                    g.nop().then_inc(s_posr, 1)
                g.nop().then_inc(s_scat_all, 1)
            with g.If(unsorted == 0):
                g.wait_ge(s_rec_out, 32)
                for j in range(BLOCKS):
                    g.indirect_dma_start(blk[:, j, :], None, rec_dram.rearrange("(n a) -> n a", a=1),
                                         bass.IndirectOffsetOnAxis(run_start[:, j:j + 1], 0))\
                        .then_inc(s_run, 16)
                g.wait_ge(s_run, 16 * BLOCKS)
                g.nop().then_inc(s_blk, 16)
            g.wait_ge(s_mask, 16)
            for L in range(LAYERS + 1):
                if L > 0:
                    g.wait_ge(S_IN["stored"], 16 * BASE[L])
                    if L == LAYERS:
                        g.wait_ge(S_IN["stored2"], 16 * TILES)
                    with g.If(late > 0):
                        g.wait_ge(S_LATE["stored"], 16 * BASE[L])
                        if L == LAYERS:
                            g.wait_ge(S_LATE["stored2"], 16 * TILES)
                table = H[L] if L < LAYERS else MSG
                with g.Fori(0, GROUPS) as i:
                    for u in range(GROUP):
                        if u % HALF == 0:
                            g.wait_ge(s_idx, i * 2 + (L * (2 * GROUPS + 1) + u // HALF + 1))
                            g.sem_inc(s_held_g, 1)
                        g.indirect_dma_start(rows[:, u, 0:D], None, table,
                                             bass.IndirectOffsetOnAxis(idx_st[:, u:u + 1], 0))\
                            .then_inc(s_rows[u], 16)

        @block.scalar
        def _(a):
            for to, frm in weights:
                a.dma_start(to, frm).then_inc(s_wts, 16)
            a.wait_ge(s_edges, 64)
            a.copy(e_f[:, :], e_dst[:, :]).then_inc(s_float, 1)
            a.wait_ge(s_wts, 16 * N_WTS)
            a.wait_ge(s_const, N_CONST)
            a.activation(bn[:, 0, :], bn[:, 0, :], ACT.Sqrt, bias=eps_col[:, :]).then_inc(s_bnsq, 1)
            for q in range(TILES // XB):
                a.wait_ge(s_lnstat, q + 1)
                a.activation(lnm[:, q % 2, :, 2:3], lnm[:, q % 2, :, 1:2], ACT.Sqrt, bias=eps_col[0:TN, :])\
                    .then_inc(s_lnsq, 1)
                a.wait_ge(s_lnr, q + 1)
                for k in range(XB):
                    i = a.activation(xs[:, q % 2, k, :], xs[:, q % 2, k, :], ACT.Relu,
                                     bias=lnm[:, q % 2, k, 0:1], scale=lnm[:, q % 2, k, 2:3])
                i.then_inc(s_lnh, 1)
            a.wait_ge(s_flags, 1)
            unsorted = a.value_load(flags[0:1, 0:1], min_val=0, max_val=1)
            late = a.value_load(flags[0:1, 1:2], min_val=0, max_val=1)
            with a.If(unsorted > 0):
                a.wait_ge(s_pos, 1)
                with a.Fori(0, EC // 8) as c:
                    a.wait_ge(s_posr, c + 1)
                    a.copy(st_pos[:, :], pos_i[:, bass.ds(c * 8, 8)]).then_inc(s_stage, 1)
                    a.copy(st_rec[:, :], e_rec[:, bass.ds(c * 8, 8)]).then_inc(s_stage, 1)
            a.wait_ge(s_table, 1)

            for L in range(LAYERS + 1):
                idx = idx0 if L < LAYERS else idx1

                def stage(i, h, L=L, idx=idx):
                    a.wait_ge(s_sum, i * GROUP + (L * CHUNKS + (h + 1) * HALF))
                    a.copy(idx_st[:, h * HALF:(h + 1) * HALF],
                           idx[:, bass.ds(i * GROUP + h * HALF, HALF)]).then_inc(s_idx, 1)

                def early(t, S):
                    act_turned(a, L, t, S)
                    if L == LAYERS - 1:
                        act_sd(a, t, S)
                    if L == LAYERS:
                        act_gates(a, t, S)

                def late_part(t, S):
                    if L == LAYERS - 1:
                        act_turned_h(a, t, S)
                        act_y1(a, t, S)
                        act_y2(a, t, S)
                    if L == LAYERS:
                        act_mlp(a, t, S, 1)
                        act_mlp(a, t, S, 2)

                a.wait_ge(s_sum, L * CHUNKS + GROUP)
                if L > 0:
                    a.wait_ge(s_idx, L * (2 * GROUPS + 1))
                stage(0, 0)
                for i in range(LEAD):
                    stage(i, 1)
                    stage(i + 1, 0)
                with a.Fori(0, TILES) as t:
                    stage(t + LEAD, 1)
                    early(t, S_IN)
                    stage(t + (LEAD + 1), 0)
                    late_part(t, S_IN)
                with a.If(late > 0):
                    with a.Fori(0, TILES) as t:
                        early(t, S_LATE)
                        late_part(t, S_LATE)

        @block.vector
        def _(v):
            dv = 0

            def step(i):
                nonlocal dv
                i.then_inc(s_dv, 1)
                dv += 1

            def own():
                v.wait_ge(s_dv, dv)

            v.wait_ge(s_const, N_CONST)
            step(v.memset(cntb[:, 0:1], 0.0))
            step(v.memset(cntb[:, TILES:TILES + 1], float(EC)))
            step(v.memset(acc[:, :], 0.0))
            v.wait_ge(s_float, 1)
            step(v.scalar_tensor_tensor(e_tmp[:, 0:EC - 1], e_f[:, 0:EC - 1], 1.0, e_f[:, 1:EC],
                                        ALU.mult, ALU.is_gt, accum_out=bad[:, 0:1]))
            own()
            step(v.tensor_copy(bad[:, 2:3], e_f[:, EC - 1:EC]))
            step(v.memset(bad[:, 1:2], 0.0))
            step(v.tensor_copy(e_nextf[0:EP - 1, :], e_next[0:EP - 1, :]))
            own()
            step(v.tensor_tensor(bad[0:EP - 1, 1:2], bad[0:EP - 1, 2:3], e_nextf[0:EP - 1, :], ALU.is_gt))
            own()
            with v.Fori(0, (TILES - 1) // 7) as c:
                for k in range(7):
                    v.tensor_scalar(e_tmp[:, :], e_f[:, :], bound[0:EP, bass.ds(c * 7 + (k + 1), 1)], 0.0,
                                    ALU.is_lt, ALU.add, accum_out=cntb[:, bass.ds(c * 7 + (k + 1), 1)])\
                        .then_inc(s_dv, 1)
                    v.wait_ge(s_dv, c * 7 + (dv + k + 1))
            dv += TILES - 1
            v.nop().then_inc(s_float, 1)
            step(v.tensor_scalar(e_rec[:, :], e_dst[:, :], DST_SHIFT, None, ALU.logical_shift_left))
            step(v.tensor_scalar(e_rel[:, :], e_rel[:, :], REL_SHIFT, None, ALU.logical_shift_left))
            own()
            step(v.tensor_tensor(e_rec[:, :], e_rec[:, :], e_rel[:, :], ALU.bitwise_or))
            own()
            v.tensor_tensor(e_rec[:, :], e_rec[:, :], e_src[:, :], ALU.bitwise_or).then_inc(s_rec, 1)

            v.wait_ge(s_pe, 1)
            step(v.tensor_copy(tl[:, 0:2], pA[0:TILES, 0:2]))
            own()
            step(v.tensor_tensor(tl[:, 2:3], tl[:, 1:2], tl[:, 0:1], ALU.subtract))
            own()
            step(v.tensor_scalar(tli[:, 0:1], tl[:, 2:3], float(P - 1), None, ALU.add))
            own()
            step(v.tensor_scalar(tli[:, 0:1], tli[:, 0:1], 7, None, ALU.arith_shift_right))
            own()
            v.tensor_scalar(tl[:, 3:4], tli[:, 0:1], 1.0, None, ALU.max).then_inc(s_chunks, 1)
            v.wait_ge(s_pe, 2)
            step(v.tensor_copy(tl[:, 4:5], pA[0:TILES, 4:5]))
            own()
            step(v.tensor_tensor(tl[:, 5:6], tl[:, 4:5], tl[:, 3:4], ALU.add))
            step(v.scalar_tensor_tensor(vals[:, 1:2], tl[:, 4:5], -float(P), tl[:, 0:1], ALU.mult, ALU.add))
            step(v.tensor_copy(vals[:, 0:1], tile_p[:, 0:1]))
            step(v.tensor_copy(vals[:, 2:3], tl[:, 1:2]))
            step(v.tensor_scalar(first[:, :], chunk_iota[:, :], tl[:, 4:5], None, ALU.is_equal))
            own()
            step(v.tensor_tensor(tl[:, 6:7], tl[:, 5:6], tile_p[:, 2:3], ALU.is_gt))
            step(v.tensor_tensor(tl[:, 7:8], tl[:, 5:6], tile_p[:, 3:4], ALU.add))
            own()
            step(v.tensor_scalar(belong[:, :], chunk_iota[:, :], tl[:, 7:8], None, ALU.is_lt))
            own()
            v.scalar_tensor_tensor(belong[:, :], chunk_iota[:, :], tl[:, 4:5], belong[:, :],
                                   ALU.is_ge, ALU.mult).then_inc(s_chunks, 1)
            v.wait_ge(s_pe, 3)
            step(v.tensor_copy(info[:, :, :], pA[:, 0:3 * BLOCKS].rearrange("p (j c) -> p j c", c=3)))
            step(v.tensor_scalar(flags[0:1, 1:2], pA[0:1, 32:33], 0.0, None, ALU.is_gt))
            step(v.tensor_copy(flagf[0:1, 0:2], pA[0:1, 34:36]))
            own()
            step(v.tensor_tensor(flagf[0:1, 2:3], flagf[0:1, 0:1], flagf[0:1, 1:2], ALU.add))
            step(v.tensor_tensor(info[:, :, 1], info[:, :, 1], chunk_start[:, :], ALU.add))
            own()
            v.tensor_scalar(flags[0:1, 0:1], flagf[0:1, 2:3], 0.0, None, ALU.is_gt).then_inc(s_dv, 1)
            dv += 1
            step(v.tensor_tensor(info[:, :, 2], info[:, :, 2], info[:, :, 1], ALU.subtract))
            step(v.tensor_scalar(run_start[:, :], info[:, :, 1], float(E), None, ALU.min))
            own()
            v.nop().then_inc(s_flags, 1)
            for h in range(2):
                step(v.tensor_copy(toff[0:1, h * CROW:(h + 1) * CROW], (pB, pC)[h][0:1, 0:CROW]))
                step(v.tensor_scalar(keep[:, h * CROW:(h + 1) * CROW], (ps[0], ps[1])[h][:, 0:CROW], -1.0, 1.0,
                                     ALU.mult, ALU.add))
            v.wait_ge(s_bnsq, 1)
            step(v.reciprocal(bn[:, 0, :], bn[:, 0, :]))
            own()
            step(v.tensor_tensor(bn[:, 1, :], bn[:, 1, :], bn[:, 0, :], ALU.mult))
            step(v.tensor_tensor(bnrow[0:1, 0, :], bnrow[0:1, 0, :], bnrow[0:1, 1, :], ALU.subtract))
            own()
            step(v.tensor_tensor(bnrow[0:1, 0, :], bnrow[0:1, 0, :], bn[0:1, 1, :], ALU.mult))
            own()
            step(v.tensor_tensor(bnrow[0:1, 0, :], bnrow[0:1, 0, :], bnrow[0:1, 2, :], ALU.add))
            for w in (wl, wr):
                for k in range(KD):
                    step(v.tensor_tensor(w[:, :, k, :], w[:, :, k, :],
                                         bn[:, 1, :].rearrange("p (l d) -> p l d", d=D), ALU.mult))
            step(v.tensor_tensor(bihc[:, 0, :], bihc[:, 0, :], bihc[:, 1, :], ALU.add))
            for q in range(TILES // XB):
                v.wait_ge(s_x[q % 2], 16 * (q // 2 + 1))
                for k in range(XB):
                    step(v.bn_stats(lns[:, k, :], xs[:, q % 2, k, :]))
                own()
                for k in range(XB):
                    i = v.bn_aggr(lnm[:, q % 2, k, 0:2], lns[:, k, :])
                i.then_inc(s_lnstat, 1)
                v.wait_ge(s_lnsq, q + 1)
                step(v.reciprocal(lnm[:, q % 2, :, 2:3], lnm[:, q % 2, :, 2:3]))
                own()
                v.scalar_tensor_tensor(lnm[:, q % 2, :, 0:1], lnm[:, q % 2, :, 0:1], -1.0,
                                       lnm[:, q % 2, :, 2:3], ALU.mult, ALU.mult).then_inc(s_lnr, 1)
            v.wait_ge(s_dv, dv)
            unsorted = v.value_load(flags[0:1, 0:1], min_val=0, max_val=1)
            late = v.value_load(flags[0:1, 1:2], min_val=0, max_val=1)
            v.wait_ge(s_lnh, TILES // XB)
            with v.If(unsorted > 0):
                v.memset(pos_f[:, :], 0.0).then_inc(s_scan, 1)
                v.tensor_tensor(ncnt[:, :], cntb[:, 1:TILES + 1], cntb[:, 0:TILES], ALU.subtract)\
                    .then_inc(s_scan, 1)
                v.tensor_scalar(diag[:, :], ident[0:TILES, 0:TILES], tl[:, 4:5], float(P), ALU.mult, ALU.mult)\
                    .then_inc(s_scan, 1)
                v.wait_ge(s_scan_pe, 1)
                v.tensor_scalar(slot0[:, :], pA[0:EP, 0:TILES], -1.0, None, ALU.add).then_inc(s_scan, 1)
                v.wait_ge(s_scan, 4)
                with v.Fori(0, TILES) as t:
                    v.tensor_scalar(e_tmp[:, :], e_f[:, :], bound[0:EP, bass.ds(t, 1)], None, ALU.is_ge)\
                        .then_inc(s_scan, 1)
                    v.wait_ge(s_scan, t * 5 + 5)
                    v.scalar_tensor_tensor(e_tmp[:, :], e_f[:, :], bound[0:EP, bass.ds(t + 1, 1)],
                                           e_tmp[:, :], ALU.is_lt, ALU.mult).then_inc(s_scan, 1)
                    v.wait_ge(s_scan, t * 5 + 6)
                    v.tensor_tensor_scan(e_scan[:, :], ones[0:EP, 0:1].to_broadcast([EP, EC]), e_tmp[:, :],
                                         slot0[:, bass.ds(t, 1)], ALU.mult, ALU.add).then_inc(s_scan, 1)
                    v.wait_ge(s_scan, t * 5 + 7)
                    v.tensor_tensor(e_scan[:, :], e_scan[:, :], e_tmp[:, :], ALU.mult).then_inc(s_scan, 1)
                    v.wait_ge(s_scan, t * 5 + 8)
                    v.tensor_tensor(pos_f[:, :], pos_f[:, :], e_scan[:, :], ALU.add).then_inc(s_scan, 1)
                    v.wait_ge(s_scan, t * 5 + 9)
                v.tensor_copy(pos_i[:, :], pos_f[:, :]).then_inc(s_pos, 1)
                v.nop().then_inc(s_posr, 1)
            v.wait_ge(s_blk, 16)
            bf = blk[:, :, :].rearrange("p j c -> p (j c)")
            step(v.tensor_scalar(u_src[:, :], bf, (1 << SRC_BITS) - 1, None, ALU.bitwise_and))
            step(v.tensor_scalar(u_dst[:, :], bf, DST_SHIFT, (1 << SRC_BITS) - 1,
                                 ALU.logical_shift_right, ALU.bitwise_and))
            step(v.tensor_scalar(u_rel[:, :], bf, REL_SHIFT, None, ALU.logical_shift_right))
            own()
            for j in range(BLOCKS):
                step(v.tensor_scalar(u_f[:, 2, j * P:(j + 1) * P], slot_iota[:, :], info[:, j, 2:3], BIG,
                                     ALU.is_ge, ALU.mult))
            step(v.scalar_tensor_tensor(u_f[:, 1, :], u_rel[:, :], float(N), u_src[:, :], ALU.mult, ALU.add))
            step(v.tensor_copy(u_f[:, 0, :], u_src[:, :]))
            own()
            for j in range(BLOCKS):
                c = slice(j * P, (j + 1) * P)
                step(v.scalar_tensor_tensor(u_f[:, 2, c], u_dst[:, c], info[:, j, 0:1], u_f[:, 2, c],
                                            ALU.subtract, ALU.add))
            own()
            v.nop().then_inc(s_unp, 1)
            n = 0
            for k, to in enumerate((idx0, idx1, dloc)):
                for h in range(2):
                    c = slice(512 * h, min(512 * (h + 1), CP))
                    v.wait_ge(s_turn, n + 1)
                    i = v.tensor_copy(to[:, c], (ps + [pA, pB])[n][:, 0:c.stop - c.start])
                    n += 1
                    i.then_inc(s_dv, 1)
                    dv += 1
            v.wait_ge(s_dv, dv)
            v.nop().then_inc(s_table, 1)
            v.nop().then_inc(s_acc0, PS)
            v.nop().then_inc(s_acc, PS)

            for L in range(LAYERS + 1):
                def chunk_head(i, L=L):
                    _, offs = nc.values_load_multi_w_load_instructions(
                        toff[0:1, bass.ds(i * GROUP, GROUP)], engines=(mybir.EngineType.DVE,),
                        min_val=0, max_val=(TILES - 1) * W,
                        skip_runtime_bounds_check_because="the table is made of offsets of tiles")
                    for h in range(2):
                        v.wait_ge(s_sum, i * GROUP + (L * CHUNKS + (h + 1) * HALF))
                        v.tensor_tensor(
                            onehot[:, h * HALF:(h + 1) * HALF, :],
                            node_iota[:, :].unsqueeze(1).to_broadcast([P, HALF, TN]),
                            dloc[:, bass.ds(i * GROUP + h * HALF, HALF)].unsqueeze(2)
                            .to_broadcast([P, HALF, TN]), ALU.is_equal).then_inc(s_hot, 1)
                    return offs

                def add(i, u, offs, L=L):
                    v.wait_ge(s_sum, i * GROUP + (L * CHUNKS + GROUP + u + 1))
                    for s_part, c0, c1 in ((s_acc0, 0, P), (s_acc, P, W)):
                        v.wait_ge(s_part, i * GROUP + (L * CHUNKS + PS + u))
                        a = acc[0:TN, bass.ds(offs[u] + c0, c1 - c0)]
                        v.scalar_tensor_tensor(a, a, keep[0:TN, bass.ds(i * GROUP + u, 1)],
                                               ps[u % PS][0:TN, c0:c1], ALU.mult, ALU.add)\
                            .then_inc(s_part, 1)

                def stages(t, S, L=L):
                    out_ = [lambda: dve_new(v, L, t, S)]
                    if L == LAYERS - 1:
                        out_.append(lambda: dve_norm(v, t, S))
                    if L == LAYERS:
                        out_.insert(0, lambda: dve_cell(v, t, S))
                    return out_

                at = {0: (8,), 2: (6, 7), 3: (7, 14)}[0 if L < LAYERS - 1 else L]

                with v.Fori(0, LEAD) as i:
                    offs = chunk_head(i)
                    for u in range(GROUP):
                        add(i, u, offs)
                with v.Fori(0, TILES) as t:
                    i = t + LEAD
                    v.wait_ge(s_acc0, i * GROUP + (L * CHUNKS + PS))
                    v.wait_ge(s_acc, i * GROUP + (L * CHUNKS + PS))
                    dve_scale(v, L, t, S_IN)
                    offs = chunk_head(i)
                    todo = stages(t, S_IN)
                    for u in range(GROUP):
                        add(i, u, offs)
                        if u in at:
                            todo[at.index(u)]()
                with v.If(late > 0):
                    v.wait_ge(s_acc0, (L + 1) * CHUNKS + PS)
                    v.wait_ge(s_acc, (L + 1) * CHUNKS + PS)
                    with v.Fori(0, TILES) as t:
                        dve_scale(v, L, t, S_LATE)
                        for s in stages(t, S_LATE):
                            s()

        @block.tensor
        def _(pe):
            pe.wait_ge(s_float, 2)
            pe.matmul(pA[0:TILES, 0:1], cntb[:, 0:TILES], ones[0:EP, 0:1], start=True, stop=True)
            pe.matmul(pA[0:TILES, 1:2], cntb[:, 1:TILES + 1], ones[0:EP, 0:1], start=True, stop=True)\
                .then_inc(s_pe, 1)
            pe.wait_ge(s_chunks, 1)
            pe.matmul(pA[0:TILES, 4:5], tri[0:TILES, 0:TILES], tl[:, 3:4], start=True, stop=True)\
                .then_inc(s_pe, 1)
            pe.wait_ge(s_chunks, 2)
            for j in range(BLOCKS):
                pe.matmul(pA[:, 3 * j:3 * j + 3], belong[:, j * P:(j + 1) * P], vals[:, :],
                          start=True, stop=True)
            pe.matmul(pA[:, 32:33], ones[0:TILES, :], tl[:, 6:7], start=True, stop=True)
            pe.matmul(pA[:, 34:36], ones[0:EP, :], bad[:, 0:2], start=True, stop=True)
            for h in range(2):
                c = slice(h * CROW, (h + 1) * CROW)
                pe.matmul((pB, pC)[h][0:1, 0:CROW], tile_p[:, 1:2], belong[:, c], start=True, stop=True)
                i = pe.matmul(ps[h][:, 0:CROW], ones[0:TILES, :], first[:, c], start=True, stop=True)
            i.then_inc(s_pe, 1)
            pe.wait_ge(s_flags, 1)
            unsorted = pe.value_load(flags[0:1, 0:1], min_val=0, max_val=1)
            late = pe.value_load(flags[0:1, 1:2], min_val=0, max_val=1)
            with pe.If(unsorted > 0):
                pe.wait_ge(s_scan, 3)
                pe.matmul(pA[0:EP, 0:TILES], tri[0:EP, 0:EP], ncnt[:, :], start=True, stop=False)
                pe.matmul(pA[0:EP, 0:TILES], ones[0:TILES, 0:EP], diag[:, :], start=False, stop=True)\
                    .then_inc(s_scan_pe, 1)
            pe.wait_ge(s_wts, 16 * N_WTS)
            pe.wait_ge(s_unp, 1)
            n = 0
            for k in range(3):
                for h in range(2):
                    c0, c1 = 512 * h, min(512 * (h + 1), CP)
                    for c in range(c0, c1, P):
                        i = pe.transpose((ps + [pA, pB])[n][:, c - c0:c - c0 + P], u_f[:, k, c:c + P],
                                         ident[:, :])
                    i.then_inc(s_turn, 1)
                    n += 1
            pe.wait_ge(s_table, 1)
            for L in range(LAYERS + 1):
                def product(i, u, L=L):
                    if u % HALF == 0:
                        pe.wait_ge(s_hot, i * 2 + (L * 2 * GROUPS + u // HALF + 1))
                    pe.wait_ge(s_rows[u], i * 16 + 16 * (L * GROUPS + 1))
                    pe.wait_ge(s_acc, i * GROUP + (L * CHUNKS + u + 1))
                    pe.matmul(ps[u % PS][0:TN, 0:W], onehot[:, u, :], rows[:, u, :], start=True, stop=True)\
                        .then_inc(s_sum, 1)

                with pe.Fori(0, LEAD) as i:
                    for u in range(GROUP):
                        product(i, u)
                with pe.Fori(0, TILES) as t:
                    todo = pe_stages(pe, L, t, S_IN)
                    for u in range(GROUP):
                        product(t + LEAD, u)
                        if u in hooks(L):
                            todo[hooks(L).index(u)]()
                with pe.If(late > 0):
                    with pe.Fori(0, TILES) as t:
                        for s in pe_stages(pe, L, t, S_LATE):
                            s()


_NAMES = ["x", "src", "dst", "edge_type_2", "L0_gnn_mask_embed", "L0_gnn_Wl", "L0_gnn_Wr", "L0_gnn_b",
          "L0_gnn_gamma", "L0_gnn_beta", "L0_gnn_rmean", "L0_gnn_rvar", "L1_gnn_W_rel", "L1_gnn_b_rel",
          "L1_gnn_W_ih", "L1_gnn_b_ih", "L1_gnn_b_hh", "L1_gnn_W1", "L1_gnn_b1", "L1_gnn_W2", "L1_gnn_b2",
          "L1_gnn_W3", "L1_gnn_b3"]
_TURNED = ("L1_gnn_W_rel", "L1_gnn_W_ih", "L1_gnn_W1", "L1_gnn_W2", "L1_gnn_W3")


def kernel(**inputs):
    import numpy as _np
    import concourse.bacc as _bacc
    from concourse import mybir as _mybir
    from concourse.bass_utils import run_bass_kernel_spmd as _run

    nc = _bacc.Bacc("TRN2", target_bir_lowering=False, num_devices=1)
    arrays, args = {}, []
    for name in _NAMES:
        a = _np.asarray(inputs[name])
        if name in _TURNED:
            a = _np.swapaxes(a, -1, -2)
        a = _np.ascontiguousarray(a)
        arrays[f"in_{name}_dram"] = a
        args.append(nc.dram_tensor(f"in_{name}_dram", a.shape, _mybir.dt.from_np(a.dtype),
                                   kind="ExternalInput").ap())
    args.append(nc.dram_tensor("out_0_dram", (N, D), _mybir.dt.float32, kind="ExternalOutput").ap())
    gnn(nc, *args)
    r = _run(nc, [arrays], core_ids=[0])
    return r.results[0]["out_0_dram"]
```

```python
from contextlib import ExitStack

import concourse.bass as bass
from concourse import mybir

F32 = mybir.dt.float32
I32 = mybir.dt.int32
ALU = mybir.AluOpType
ACT = mybir.ActivationFunctionType

N, E, D = 6250, 100000, 256
P = 128
KD = D // P
TN = 125
TILES = N // TN
EP, EC = 125, E // 125
GROUP = 16
HALF = GROUP // 2
CHUNKS = -(-(E // P + TILES) // GROUP) * GROUP
GROUPS = CHUNKS // GROUP
BLOCKS = -(-CHUNKS // P)
CP = BLOCKS * P
LEAD = GROUPS - TILES
W = D + 1
CROW = CP // 2
STAGED = 2 * (GROUPS + 1)
PS = 4
LAYERS = 3
EPS = 1e-5
SRC_BITS = 13
DST_SHIFT, REL_SHIFT = SRC_BITS, 2 * SRC_BITS
BIG = float(1 << 20)
XB = 5
assert TN * TILES == N and EP * EC == E and CHUNKS * P >= E + TILES * P and LEAD >= 1
PE_AT = [(4, 6), (2, 4), (2, 4, 12, 13, 15), (2, 4, 12, 13, 14)]
DVE_AT = [(0, 1, 2, 8), (0, 7), (0, 1, 5, 6, 7, 9, 10), (0, 9, 10, 15)]
HOT_AT = (3, 12)


def gnn(nc, x, src, dst, rel, mask_embed, Wl, Wr, b, gamma, beta, rmean, rvar,
        WrelT, b_rel, WihT, b_ih, b_hh, W1T, b1, W2T, b2, W3T, b3, out):
    ctx = ExitStack()
    with ctx:
        ctx.enter_context(nc.allow_non_contiguous_dma(reason="bias columns and row ends: a few elements"))

        def sb(name, shape, dt=F32):
            return ctx.enter_context(nc.sbuf_tensor(name, shape, dt))

        def sem(name):
            return ctx.enter_context(nc.semaphore(name))

        rec_dram = nc.dram_tensor("rec_dram", (E + P,), I32, kind="Internal").ap()
        slot_dram = nc.dram_tensor("slot_dram", (CP * P,), I32, kind="Internal").ap()
        H = [nc.dram_tensor(f"h{i}_dram", (N, D), F32, kind="Internal").ap() for i in range(LAYERS)]
        X1 = nc.dram_tensor("x1_dram", (N, D), F32, kind="Internal").ap()
        MSG = nc.dram_tensor("msg_dram", (2 * N, D), F32, kind="Internal").ap()

        ident = sb("ident", [P, P])
        ones = sb("ones", [P, P])
        tri = sb("tri", [P, P])
        node_iota = sb("node_iota", [P, TN])
        slot_iota = sb("slot_iota", [P, P])
        chunk_iota = sb("chunk_iota", [TILES, CP])
        chunk_start = sb("chunk_start", [P, BLOCKS])
        bound = sb("bound", [P, TILES + 1])
        tile_p = sb("tile_p", [TILES, 3])
        eps_col = sb("eps_col", [P, 1])
        wl = sb("wl", [P, LAYERS, KD, D])
        wr = sb("wr", [P, LAYERS, KD, D])
        bn = sb("bn", [P, 2, LAYERS * D])
        bnrow = sb("bnrow", [1, 3, LAYERS * D])
        wrel = sb("wrel", [P, 2, KD, D])
        brelc = sb("brelc", [P, 2, KD])
        brelr = sb("brelr", [1, 2, D])
        wih = sb("wih", [P, KD, 4 * D])
        bihc = sb("bihc", [P, 2, 8])
        w1 = sb("w1", [P, KD, P])
        w2 = sb("w2", [P, P])
        w3 = sb("w3", [P, D])
        b12 = sb("b12", [P, 2])
        b3r = sb("b3r", [1, D])
        idx0 = sb("idx0", [P, CP], I32)
        idx1 = sb("idx1", [P, CP], I32)
        dloc = sb("dloc", [P, CP])
        keep = sb("keep", [P, CP])
        toff = sb("toff", [1, CP], I32)
        flags = sb("flags", [1, 2], I32)
        acc = sb("acc", [P, (TILES + 1) * W])
        rows = sb("rows", [P, GROUP, W])
        onehot = sb("onehot", [P, GROUP, TN])
        idx_st = sb("idx_st", [P, GROUP], I32)
        deg = sb("deg", [P, 1])
        rdeg = sb("rdeg", [P, TILES])
        aggn = sb("aggn", [P, D])
        ht = sb("ht", [P, D])
        xt = sb("xt", [P, D])
        tT = sb("tT", [P, 4, TN])
        hn = sb("hn", [P, D])
        x1t = sb("x1t", [P, D])
        stat = sb("stat", [P, 12])
        y1 = sb("y1", [P, 4, TN])
        msg = sb("msg", [P, 2, D])
        gate = sb("gate", [P, 6, TN])
        cell = sb("cell", [P, 2, 2, TN])
        z12 = sb("z12", [P, 2, TN])

        e_dst = sb("e_dst", [EP, EC], I32)
        e_src = sb("e_src", [EP, EC], I32)
        e_rel = sb("e_rel", [EP, EC], I32)
        e_rec = sb("e_rec", [EP, EC], I32)
        e_f = sb("e_f", [EP, EC])
        e_next = sb("e_next", [EP, 1], I32)
        e_nextf = sb("e_nextf", [EP, 1])
        bad = sb("bad", [EP, 3])
        cntb = sb("cntb", [EP, TILES + 1])
        zero_i = sb("zero_i", [P, P], I32)
        tl = sb("tl", [TILES, 8])
        tli = sb("tli", [TILES, 1], I32)
        vals = sb("vals", [TILES, 3])
        info = sb("info", [P, BLOCKS, 3])
        run_start = sb("run_start", [P, BLOCKS], I32)
        flagf = sb("flagf", [1, 3])
        blk = sb("blk", [P, BLOCKS, P], I32)
        xs = sb("xs", [TN, 2, XB, D])
        lns = sb("lns", [TN, XB, 6])
        lnm = sb("lnm", [TN, 2, XB, 3])
        e_tmp = sb("e_tmp", [EP, EC])
        st_pos = sb("st_pos", [EP, 8], I32)
        st_rec = sb("st_rec", [EP, 8], I32)
        ncnt = sb("ncnt", [EP, TILES])
        diag = sb("diag", [TILES, TILES])
        slot0 = sb("slot0", [EP, TILES])
        belong = acc[0:TILES, 0:CP]
        first = acc[0:TILES, CP:2 * CP]
        u_rel = acc[:, 2 * CP:3 * CP].bitcast(I32)
        u_f = acc[:, 3 * CP:6 * CP].rearrange("p (k c) -> p k c", k=3)
        e_scan = u_f[0:EP, 0, 0:EC]
        pos_f = u_f[0:EP, 1, 0:EC]
        pos_i = u_f[0:EP, 2, 0:EC].bitcast(I32)
        hot_i = onehot[:, :, :].rearrange("p a b -> p (a b)").bitcast(I32)
        u_src = hot_i[:, 0:CP]
        u_dst = hot_i[:, CP:2 * CP]

        weights = []
        lay = "l (k p) n -> p l k n"
        weights.append((bn[:, 0, :], rvar.rearrange("l d -> (l d)").partition_broadcast(P)))
        weights.append((bn[:, 1, :], gamma.rearrange("l d -> (l d)").partition_broadcast(P)))
        for k, w in enumerate((b, rmean, beta)):
            weights.append((bnrow[0:1, k, :], w.rearrange("(a l) d -> a (l d)", a=1)))
        weights.append((wl[:, :, :, :], Wl.rearrange(lay, p=P)))
        weights.append((wr[:, :, :, :], Wr.rearrange(lay, p=P)))
        weights.append((wrel[:, :, :, :], WrelT.rearrange(lay, p=P)))
        weights.append((brelc[:, :, :], b_rel.rearrange("r (k p) -> p r k", p=P)))
        weights.append((brelr[:, :, :], b_rel.rearrange("(a r) d -> a r d", a=1)))
        weights.append((wih[:, :, :], WihT.rearrange("(k p) n -> p k n", p=P)))
        weights.append((bihc[:, 0, :], b_ih.rearrange("(c p) -> p c", p=P)))
        weights.append((bihc[:, 1, :], b_hh.rearrange("(c p) -> p c", p=P)))
        weights.append((w1[:, :, :], W1T.rearrange("(k p) n -> p k n", p=P)))
        weights.append((w2[:, :], W2T))
        weights.append((w3[:, :], W3T))
        weights.append((b12[:, 0:1], b1.rearrange("(p a) -> p a", a=1)))
        weights.append((b12[:, 1:2], b2.rearrange("(p a) -> p a", a=1)))
        weights.append((b3r[0:1, :], b3.rearrange("(a d) -> a d", a=1)))
        N_WTS = len(weights)
        N_CONST = 14

        def bank(name):
            return ctx.enter_context(nc.psum_tensor(name, [P, 512], F32))

        ps = [bank(f"ps{i}") for i in range(PS)]
        pA, pB, pC, pD = bank("pA"), bank("pB"), bank("pC"), bank("pD")

        s_const = sem("s_const")
        s_wts = sem("s_wts")
        s_edges = sem("s_edges")
        s_float = sem("s_float")
        s_rec = sem("s_rec")
        s_rec_out = sem("s_rec_out")
        s_dv = sem("s_dv")
        s_pe = sem("s_pe")
        s_blk = sem("s_blk")
        s_flags = sem("s_flags")
        s_fill = sem("s_fill")
        s_posr = sem("s_posr")
        s_stage = sem("s_stage")
        s_scat = sem("s_scat")
        s_scat_all = sem("s_scat_all")
        s_pos = sem("s_pos")
        s_run = sem("s_run")
        s_chunks = sem("s_chunks")
        s_scan = sem("s_scan")
        s_scan_pe = sem("s_scan_pe")
        s_unp = sem("s_unp")
        s_turn = sem("s_turn")
        s_x = [sem("s_x0"), sem("s_x1")]
        s_lnstat = sem("s_lnstat")
        s_lnsq = sem("s_lnsq")
        s_lnr = sem("s_lnr")
        s_lnh = sem("s_lnh")
        s_h0 = [sem("s_h00"), sem("s_h01")]
        s_mask = sem("s_mask")
        s_bn = sem("s_bn")
        s_bnsq = sem("s_bnsq")
        s_table = sem("s_table")
        s_held_v = sem("s_held_v")
        s_held_s = sem("s_held_s")
        s_held_g = sem("s_held_g")
        s_idx = sem("s_idx")
        s_rows = [sem(f"s_rows{u}") for u in range(GROUP)]
        s_hot = sem("s_hot")
        s_sum = sem("s_sum")
        s_acc0 = sem("s_acc0")
        s_acc = sem("s_acc")

        def dense_sems(n):
            names = ("loaded", "xloaded", "deg", "res", "scaled", "tr", "trc", "z", "new", "stored", "stored2", "msgfree",
                     "var", "sd", "rstd", "norm", "trh", "trhc", "y1", "y1c", "y2", "y2c",
                     "gates", "gatec", "cell", "cellt", "hid", "w1", "w1c", "w2", "w2c")
            return {k: sem(f"s_{n}_{k}") for k in names}

        S_IN = dense_sems("in")
        S_LATE = dense_sems("late")

        block = ctx.enter_context(nc.Block())

        BASE = {L: L * TILES for L in range(LAYERS + 1)}

        def tile_rows(t):
            return bass.ds(t * TN, TN)

        def sp_load(sp, L, t, S):
            if L < LAYERS:
                sp.dma_start(ht[0:TN, :], H[L][tile_rows(t), :]).then_inc(S["loaded"], 16)
            else:
                sp.dma_start(xt[0:TN, :], X1[tile_rows(t), :]).then_inc(S["loaded"], 16)
            if L == LAYERS - 1:
                sp.dma_start(xt[0:TN, :], x[tile_rows(t), :]).then_inc(S["xloaded"], 16)

        def sp_store(sp, L, t, S, more):
            n = BASE[L]
            sp.wait_ge(S["new"], t + (n + 1))
            if L == LAYERS - 1:
                sp.dma_start(X1[tile_rows(t), :], x1t[0:TN, :]).then_inc(S["stored"], 16)
                if more:
                    sp_load(sp, L, t + 1, S)
                sp.wait_ge(S["y2c"], t + 1)
                sp.dma_start(MSG.rearrange("(r n) d -> n r d", r=2)[tile_rows(t), :, :],
                             msg[0:TN, :, :]).then_inc(S["stored2"], 16)
                sp.wait_ge(S["stored2"], t * 16 + 16)
                sp.sem_inc(S["msgfree"], 1)
            else:
                to = H[L + 1] if L < LAYERS - 1 else out
                sp.dma_start(to[tile_rows(t), :], hn[0:TN, :]).then_inc(S["stored"], 16)
                sp.wait_ge(S["stored"], t * 16 + 16 * (n + 1))
                sp.sem_inc(s_held_s, 1)
                if more:
                    sp_load(sp, L, t + 1, S)

        def sp_dense(sp, L, S):
            sp_load(sp, L, 0, S)
            if L == LAYERS - 1:
                sp.sem_inc(S["msgfree"], 1)
            with sp.Fori(0, TILES - 1) as t:
                sp_store(sp, L, t, S, True)
            sp_store(sp, L, TILES - 1, S, False)

        def dve_stages(v, L, t, S):
            n = BASE[L]
            a = acc[0:TN, bass.ds(t * W, D)]
            inv = rdeg[0:TN, bass.ds(t, 1)]

            def degree():
                v.tensor_scalar(deg[0:TN, :], acc[0:TN, bass.ds(t * W + D, 1)], 1.0, None, ALU.max)\
                    .then_inc(S["deg"], 1)

            def inverse():
                v.wait_ge(S["deg"], t * 2 + 1)
                v.reciprocal(inv, deg[0:TN, :]).then_inc(S["deg"], 1)

            def scale():
                if L == 0:
                    v.wait_ge(S["deg"], t * 2 + 2)
                if L < LAYERS:
                    v.tensor_scalar(aggn[0:TN, :], a, inv, None, ALU.mult).then_inc(S["scaled"], 1)
                else:
                    v.tensor_copy(aggn[0:TN, :], a).then_inc(S["scaled"], 1)

            def old():
                v.wait_ge(S["loaded"], t * 16 + 16 * (n + 1))
                v.wait_ge(S["xloaded"], t * 16 + 16)
                v.tensor_tensor(xt[0:TN, :], ht[0:TN, :], xt[0:TN, :], ALU.add).then_inc(S["res"], 1)

            def new():
                v.wait_ge(S["z"], t + (n + 1))
                if L < LAYERS - 1:
                    v.wait_ge(S["loaded"], t * 16 + 16 * (n + 1))
                    v.scalar_tensor_tensor(hn[0:TN, :], pB[0:TN, 0:D], 0.0, ht[0:TN, :], ALU.max, ALU.add)\
                        .then_inc(S["new"], 1)
                elif L == LAYERS - 1:
                    v.wait_ge(S["res"], t + 1)
                    v.wait_ge(S["stored"], t * 16 + 16 * n)
                    v.tensor_tensor(x1t[0:TN, :], pB[0:TN, 0:D], xt[0:TN, :], ALU.add)\
                        .then_inc(S["new"], 1)
                else:
                    v.wait_ge(S["loaded"], t * 16 + 16 * (n + 1))
                    v.tensor_tensor(hn[0:TN, :], pB[0:TN, 0:D], xt[0:TN, :], ALU.add)\
                        .then_inc(S["new"], 1)

            def stats():
                v.wait_ge(S["new"], t + (n + 1))
                v.bn_stats(stat[0:TN, 0:6], x1t[0:TN, :]).then_inc(S["var"], 1)

            def variance():
                v.wait_ge(S["var"], t * 2 + 1)
                v.sem_inc(s_held_v, 1)
                v.bn_aggr(stat[0:TN, 6:8], stat[0:TN, 0:6]).then_inc(S["var"], 1)

            def rstd():
                v.wait_ge(S["sd"], t + 1)
                v.reciprocal(stat[0:TN, 9:10], stat[0:TN, 8:9]).then_inc(S["rstd"], 1)

            def norm():
                v.wait_ge(S["rstd"], t + 1)
                v.tensor_scalar(hn[0:TN, :], x1t[0:TN, :], stat[0:TN, 6:7], stat[0:TN, 9:10],
                                ALU.subtract, ALU.mult).then_inc(S["norm"], 1)

            def cells():
                v.wait_ge(S["gatec"], t + 1)
                v.tensor_tensor(cell[:, 0, :, :], gate[:, 0:2, :], gate[:, 2:4, :], ALU.mult)\
                    .then_inc(S["cell"], 1)

            def hidden():
                v.wait_ge(S["cellt"], t + 1)
                v.tensor_tensor(cell[:, 0, :, :], gate[:, 4:6, :], cell[:, 1, :, :], ALU.mult)\
                    .then_inc(S["hid"], 1)

            if L == 0:
                return [degree, inverse, scale, new]
            if L < LAYERS - 1:
                return [scale, new]
            if L == LAYERS - 1:
                return [scale, old, new, stats, variance, rstd, norm]
            return [scale, cells, hidden, new]

        def act_turned(a, L, t, S):
            a.wait_ge(S["tr"], t + (BASE[L] + 1))
            k = 4 if L < LAYERS else 2
            a.copy(tT[:, 0:k, :], pA[:, 0:k * TN].rearrange("p (k n) -> p k n", k=k)).then_inc(S["trc"], 1)

        def act_sd(a, t, S):
            a.wait_ge(S["var"], t * 2 + 2)
            a.activation(stat[0:TN, 8:9], stat[0:TN, 7:8], ACT.Sqrt, bias=eps_col[0:TN, :])\
                .then_inc(S["sd"], 1)

        def act_turned_h(a, t, S):
            a.wait_ge(S["trh"], t + 1)
            a.activation(tT[:, 0:2, :], pA[:, 0:2 * TN].rearrange("p (k n) -> p k n", k=2), ACT.Relu)\
                .then_inc(S["trhc"], 1)

        def act_y1(a, t, S):
            a.wait_ge(S["y1"], t + 1)
            for q in range(4):
                i = a.activation(y1[:, q, :], pC[:, q * TN:(q + 1) * TN], ACT.Relu,
                                 bias=brelc[:, q // 2, q % 2:q % 2 + 1])
            i.then_inc(S["y1c"], 1)

        def act_y2(a, t, S):
            a.wait_ge(S["msgfree"], t + 1)
            a.wait_ge(S["y2"], t + 1)
            a.activation(msg[0:TN, :, :], pD[0:TN, :].rearrange("p (r d) -> p r d", r=2), ACT.Relu)\
                .then_inc(S["y2c"], 1)

        def act_gates(a, t, S):
            a.wait_ge(S["gates"], t + 1)
            for q, (c, f) in enumerate(((0, ACT.Sigmoid), (1, ACT.Sigmoid), (4, ACT.Tanh),
                                        (5, ACT.Tanh), (6, ACT.Sigmoid), (7, ACT.Sigmoid))):
                p = pB[:, q * TN:(q + 1) * TN] if q < 4 else pC[:, (q - 4) * TN:(q - 3) * TN]
                i = a.activation(gate[:, q, :], p, f, bias=bihc[:, 0, c:c + 1])
            i.then_inc(S["gatec"], 1)
            a.wait_ge(S["cell"], t + 1)
            a.activation(cell[:, 1, :, :], cell[:, 0, :, :], ACT.Tanh).then_inc(S["cellt"], 1)

        def act_mlp(a, t, S, k):
            a.wait_ge(S[f"w{k}"], t + 1)
            a.activation(z12[:, k - 1, :], pD[:, (k - 1) * P:(k - 1) * P + TN], ACT.Relu,
                         bias=b12[:, k - 1:k]).then_inc(S[f"w{k}c"], 1)

        def pe_turn(pe, L, t, S):
            n = BASE[L]
            pe.wait_ge(S["scaled"], t + (n + 1))
            if L < LAYERS:
                pe.wait_ge(S["loaded"], t * 16 + 16 * (n + 1))
            for k in range(4 if L < LAYERS else 2):
                frm = aggn if k < 2 else ht
                i = pe.transpose(pA[:, k * TN:(k + 1) * TN], frm[0:TN, (k % 2) * P:(k % 2 + 1) * P],
                                 ident[0:TN, 0:TN])
            i.then_inc(S["tr"], 1)

        def pe_z(pe, L, t, S):
            pe.wait_ge(S["trc"], t + (BASE[L] + 1))
            for k in range(4):
                w = (wl if k < 2 else wr)[:, L, k % 2, :]
                pe.matmul(pB[0:TN, 0:D], tT[:, k, :], w, start=(k == 0), stop=False)
            pe.matmul(pB[0:TN, 0:D], ones[0:1, 0:TN], bnrow[0:1, 0, L * D:(L + 1) * D],
                      start=False, stop=True).then_inc(S["z"], 1)

        def pe_turn_h(pe, t, S):
            pe.wait_ge(S["norm"], t + 1)
            for k in range(2):
                i = pe.transpose(pA[:, k * TN:(k + 1) * TN], hn[0:TN, k * P:(k + 1) * P], ident[0:TN, 0:TN])
            i.then_inc(S["trh"], 1)

        def pe_y1(pe, t, S):
            pe.wait_ge(S["trhc"], t + 1)
            for q in range(4):
                r, m = q // 2, q % 2
                for k in range(2):
                    i = pe.matmul(pC[:, q * TN:(q + 1) * TN], wrel[:, r, k, m * P:(m + 1) * P],
                                  tT[:, k, :], start=(k == 0), stop=(k == 1))
            i.then_inc(S["y1"], 1)

        def pe_y2(pe, t, S):
            pe.wait_ge(S["y1c"], t + 1)
            for r in range(2):
                o = pD[0:TN, r * D:(r + 1) * D]
                for k in range(2):
                    pe.matmul(o, y1[:, 2 * r + k, :], wrel[:, r, k, :], start=(k == 0), stop=False)
                i = pe.matmul(o, ones[0:1, 0:TN], brelr[0:1, r, :], start=False, stop=True)
            i.then_inc(S["y2"], 1)

        def pe_gates(pe, t, S):
            pe.wait_ge(S["trc"], t + (BASE[LAYERS] + 1))
            for q, c in enumerate((0, 1, 4, 5, 6, 7)):
                o = pB[:, q * TN:(q + 1) * TN] if q < 4 else pC[:, (q - 4) * TN:(q - 3) * TN]
                for k in range(2):
                    i = pe.matmul(o, wih[:, k, c * P:(c + 1) * P], tT[:, k, :],
                                  start=(k == 0), stop=(k == 1))
            i.then_inc(S["gates"], 1)

        def pe_w1(pe, t, S):
            pe.wait_ge(S["hid"], t + 1)
            for k in range(2):
                i = pe.matmul(pD[:, 0:TN], w1[:, k, :], cell[:, 0, k, :], start=(k == 0), stop=(k == 1))
            i.then_inc(S["w1"], 1)

        def pe_w2(pe, t, S):
            pe.wait_ge(S["w1c"], t + 1)
            pe.matmul(pD[:, P:P + TN], w2[:, :], z12[:, 0, :], start=True, stop=True).then_inc(S["w2"], 1)

        def pe_w3(pe, t, S):
            pe.wait_ge(S["w2c"], t + 1)
            pe.matmul(pB[0:TN, 0:D], z12[:, 1, :], w3[:, :], start=True, stop=False)
            pe.matmul(pB[0:TN, 0:D], ones[0:1, 0:TN], b3r[0:1, :], start=False, stop=True)\
                .then_inc(S["z"], 1)

        def pe_stages(pe, L, t, S):
            if L < LAYERS - 1:
                return [lambda: pe_turn(pe, L, t, S), lambda: pe_z(pe, L, t, S)]
            if L == LAYERS - 1:
                return [lambda: pe_turn(pe, L, t, S), lambda: pe_z(pe, L, t, S),
                        lambda: pe_turn_h(pe, t, S), lambda: pe_y1(pe, t, S), lambda: pe_y2(pe, t, S)]
            return [lambda: pe_turn(pe, L, t, S), lambda: pe_gates(pe, t, S),
                    lambda: pe_w1(pe, t, S), lambda: pe_w2(pe, t, S), lambda: pe_w3(pe, t, S)]

        @block.sync
        def _(sp):
            sp.dma_start(e_dst[:, :], dst.rearrange("(p c) -> p c", c=EC)).then_inc(s_edges, 16)
            sp.dma_start(e_next[0:EP - 1, :], dst.rearrange("(p c) -> p c", c=EC)[1:EP, 0:1])\
                .then_inc(s_edges, 16)
            sp.dma_start(e_src[:, :], src.rearrange("(p c) -> p c", c=EC)).then_inc(s_edges, 16)
            sp.dma_start(e_rel[:, :], rel.rearrange("(p c) -> p c", c=EC)).then_inc(s_edges, 16)
            xv = x.rearrange("(q t p) d -> q p t d", p=TN, t=XB)
            hv = H[0].rearrange("(q t p) d -> q p t d", p=TN, t=XB)
            for q in range(TILES // XB):
                if q >= 2:
                    sp.wait_ge(s_h0[q % 2], 16 * (q // 2))
                sp.dma_start(xs[:, q % 2, :, :], xv[q, :, :, :]).then_inc(s_x[q % 2], 16)
                if q >= 1:
                    sp.wait_ge(s_lnh, q)
                    sp.dma_start(hv[q - 1, :, :, :], xs[:, (q - 1) % 2, :, :])\
                        .then_inc(s_h0[(q - 1) % 2], 16)
            q = TILES // XB
            sp.wait_ge(s_lnh, q)
            sp.dma_start(hv[q - 1, :, :, :], xs[:, (q - 1) % 2, :, :]).then_inc(s_h0[(q - 1) % 2], 16)
            for k in range(2):
                sp.wait_ge(s_h0[k], 16 * (q // 2))
            sp.dma_start(H[0][0:1, :], mask_embed.rearrange("(a d) -> a d", a=1)).then_inc(s_mask, 16)
            sp.wait_ge(s_mask, 16)
            sp.wait_ge(s_rec, 1)
            sp.dma_start(rec_dram[0:E].rearrange("(p c) -> p c", c=EC), e_rec[:, :]).then_inc(s_rec_out, 16)
            sp.dma_start(rec_dram[E:E + P].rearrange("(a d) -> a d", a=1), zero_i[0:1, :])\
                .then_inc(s_rec_out, 16)
            sp.wait_ge(s_rec_out, 32)
            sp.wait_ge(s_flags, 1)
            unsorted = sp.value_load(flags[0:1, 0:1], min_val=0, max_val=1)
            late = sp.value_load(flags[0:1, 1:2], min_val=0, max_val=1)
            with sp.If(unsorted > 0):
                sv = slot_dram.rearrange("(j p c) -> j p c", p=P, c=P)
                for j in range(BLOCKS):
                    sp.dma_start(sv[j, :, :], zero_i[:, :]).then_inc(s_fill, 16)
                sp.wait_ge(s_fill, 16 * BLOCKS)
                sp.wait_ge(s_scat_all, 1)
                sp.dma_start(blk[:, :, :], slot_dram.rearrange("(j p c) -> p j c", p=P, c=P))\
                    .then_inc(s_blk, 16)
                sp.wait_ge(s_blk, 16)
            for L in range(LAYERS + 1):
                sp_dense(sp, L, S_IN)
                with sp.If(late > 0):
                    sp_dense(sp, L, S_LATE)

        @block.gpsimd
        def _(g):
            g.memset(ones[:, :], 1.0).then_inc(s_const, 1)
            g.memset(ident[:, :], 0.0).then_inc(s_const, 1)
            g.memset(eps_col[:, :], EPS).then_inc(s_const, 1)
            g.memset(zero_i[:, :], 0).then_inc(s_const, 1)
            g.wait_ge(s_const, 4)
            g.affine_select(out=ident[:, :], in_=ident[:, :], compare_op=ALU.not_equal, fill=1.0, base=0,
                            pattern=[[-1, P]], channel_multiplier=1).then_inc(s_const, 1)
            g.affine_select(out=tri[:, :], in_=ones[:, :], compare_op=ALU.is_gt, fill=0.0, base=0,
                            pattern=[[1, P]], channel_multiplier=-1).then_inc(s_const, 1)

            def iota(ap, pattern, base, cm):
                g.iota(ap, pattern=pattern, base=base, channel_multiplier=cm,
                       allow_small_or_imprecise_dtypes=True).then_inc(s_const, 1)

            iota(bound[:, :], [[TN, TILES + 1]], 0, 0)
            iota(node_iota[:, :], [[1, TN]], 0, 0)
            iota(slot_iota[:, :], [[1, P]], 0, 0)
            iota(chunk_iota[:, :], [[1, CP]], 0, 0)
            iota(chunk_start[:, :], [[P * P, BLOCKS]], 0, P)
            iota(tile_p[:, 0:1], [[0, 1]], 0, TN)
            iota(tile_p[:, 1:2], [[0, 1]], -TILES * W, W)
            iota(tile_p[:, 2:3], [[0, 1]], GROUP * LEAD, GROUP)
            g.memset(rows[:, :, :], 1.0).then_inc(s_sum, GROUP)
            g.wait_ge(s_flags, 1)
            unsorted = g.value_load(flags[0:1, 0:1], min_val=0, max_val=1)
            late = g.value_load(flags[0:1, 1:2], min_val=0, max_val=1)
            with g.If(unsorted > 0):
                g.wait_ge(s_fill, 16 * BLOCKS)
                with g.Fori(0, EC // 8) as c:
                    g.wait_ge(s_stage, c * 2 + 2)
                    g.sem_inc(s_held_g, 1)
                    for k in range(8):
                        g.indirect_dma_start(
                            slot_dram.rearrange("(n a) -> n a", a=1),
                            bass.IndirectOffsetOnAxis(st_pos[:, k:k + 1], 0),
                            st_rec[:, k:k + 1], None).then_inc(s_scat, 16)
                    g.wait_ge(s_scat, c * 128 + 128)
                    g.nop().then_inc(s_posr, 1)
                g.nop().then_inc(s_scat_all, 1)
            with g.If(unsorted == 0):
                g.wait_ge(s_rec_out, 32)
                for j in range(BLOCKS):
                    g.indirect_dma_start(blk[:, j, :], None, rec_dram.rearrange("(n a) -> n a", a=1),
                                         bass.IndirectOffsetOnAxis(run_start[:, j:j + 1], 0))\
                        .then_inc(s_run, 16)
                g.wait_ge(s_run, 16 * BLOCKS)
                g.nop().then_inc(s_blk, 16)
            g.wait_ge(s_mask, 16)
            for L in range(LAYERS + 1):
                if L > 0:
                    g.wait_ge(S_IN["stored"], 16 * BASE[L])
                    if L == LAYERS:
                        g.wait_ge(S_IN["stored2"], 16 * TILES)
                    with g.If(late > 0):
                        g.wait_ge(S_LATE["stored"], 16 * BASE[L])
                        if L == LAYERS:
                            g.wait_ge(S_LATE["stored2"], 16 * TILES)
                table = H[L] if L < LAYERS else MSG
                with g.Fori(0, GROUPS) as i:
                    for u in range(GROUP):
                        if u % HALF == 0:
                            g.wait_ge(s_idx, i * 2 + (L * STAGED + u // HALF + 1))
                            g.sem_inc(s_held_g, 1)
                        g.indirect_dma_start(rows[:, u, 0:D], None, table,
                                             bass.IndirectOffsetOnAxis(idx_st[:, u:u + 1], 0))\
                            .then_inc(s_rows[u], 16)

        @block.scalar
        def _(a):
            for to, frm in weights:
                a.dma_start(to, frm).then_inc(s_wts, 16)
            a.wait_ge(s_edges, 64)
            a.copy(e_f[:, :], e_dst[:, :]).then_inc(s_float, 1)
            a.wait_ge(s_wts, 16 * N_WTS)
            a.wait_ge(s_const, N_CONST)
            a.activation(bn[:, 0, :], bn[:, 0, :], ACT.Sqrt, bias=eps_col[:, :]).then_inc(s_bnsq, 1)
            for q in range(TILES // XB):
                a.wait_ge(s_lnstat, q + 1)
                a.activation(lnm[:, q % 2, :, 2:3], lnm[:, q % 2, :, 1:2], ACT.Sqrt, bias=eps_col[0:TN, :])\
                    .then_inc(s_lnsq, 1)
                a.wait_ge(s_lnr, q + 1)
                for k in range(XB):
                    i = a.activation(xs[:, q % 2, k, :], xs[:, q % 2, k, :], ACT.Relu,
                                     bias=lnm[:, q % 2, k, 0:1], scale=lnm[:, q % 2, k, 2:3])
                i.then_inc(s_lnh, 1)
            a.wait_ge(s_flags, 1)
            unsorted = a.value_load(flags[0:1, 0:1], min_val=0, max_val=1)
            late = a.value_load(flags[0:1, 1:2], min_val=0, max_val=1)
            with a.If(unsorted > 0):
                a.wait_ge(s_pos, 1)
                with a.Fori(0, EC // 8) as c:
                    a.wait_ge(s_posr, c + 1)
                    a.copy(st_pos[:, :], pos_i[:, bass.ds(c * 8, 8)]).then_inc(s_stage, 1)
                    a.copy(st_rec[:, :], e_rec[:, bass.ds(c * 8, 8)]).then_inc(s_stage, 1)
            a.wait_ge(s_table, 1)

            for L in range(LAYERS + 1):
                idx = idx0 if L < LAYERS else idx1

                def stage(i, h, L=L, idx=idx):
                    a.wait_ge(s_sum, i * GROUP + (L * CHUNKS + (h + 1) * HALF))
                    a.copy(idx_st[:, h * HALF:(h + 1) * HALF],
                           idx[:, bass.ds(i * GROUP + h * HALF, HALF)]).then_inc(s_idx, 1)

                def early(t, S):
                    act_turned(a, L, t, S)
                    if L == LAYERS - 1:
                        act_sd(a, t, S)
                    if L == LAYERS:
                        act_gates(a, t, S)

                def middle(t, S):
                    if L == LAYERS - 1:
                        act_turned_h(a, t, S)
                        act_y1(a, t, S)
                    if L == LAYERS:
                        act_mlp(a, t, S, 1)
                        act_mlp(a, t, S, 2)

                def last(t, S):
                    if L == LAYERS - 1:
                        act_y2(a, t, S)

                a.wait_ge(s_sum, L * CHUNKS + GROUP)
                if L > 0:
                    a.wait_ge(s_idx, L * STAGED)
                stage(0, 0)
                stage(0, 1)
                for i in range(LEAD):
                    stage(i + 1, 0)
                    stage(i + 1, 1)
                with a.Fori(0, TILES) as t:
                    early(t, S_IN)
                    stage(t + (LEAD + 1), 0)
                    middle(t, S_IN)
                    stage(t + (LEAD + 1), 1)
                    last(t, S_IN)
                with a.If(late > 0):
                    with a.Fori(0, TILES) as t:
                        early(t, S_LATE)
                        middle(t, S_LATE)
                        last(t, S_LATE)

        @block.vector
        def _(v):
            dv = 0

            def step(i):
                nonlocal dv
                i.then_inc(s_dv, 1)
                dv += 1

            def own():
                v.wait_ge(s_dv, dv)

            v.wait_ge(s_const, N_CONST)
            step(v.memset(cntb[:, 0:1], 0.0))
            step(v.memset(cntb[:, TILES:TILES + 1], float(EC)))
            step(v.memset(acc[:, :], 0.0))
            v.wait_ge(s_float, 1)
            step(v.scalar_tensor_tensor(e_tmp[:, 0:EC - 1], e_f[:, 0:EC - 1], 1.0, e_f[:, 1:EC],
                                        ALU.mult, ALU.is_gt, accum_out=bad[:, 0:1]))
            own()
            step(v.tensor_copy(bad[:, 2:3], e_f[:, EC - 1:EC]))
            step(v.memset(bad[:, 1:2], 0.0))
            step(v.tensor_copy(e_nextf[0:EP - 1, :], e_next[0:EP - 1, :]))
            own()
            step(v.tensor_tensor(bad[0:EP - 1, 1:2], bad[0:EP - 1, 2:3], e_nextf[0:EP - 1, :], ALU.is_gt))
            own()
            with v.Fori(0, (TILES - 1) // 7) as c:
                for k in range(7):
                    v.tensor_scalar(e_tmp[:, :], e_f[:, :], bound[0:EP, bass.ds(c * 7 + (k + 1), 1)], 0.0,
                                    ALU.is_lt, ALU.add, accum_out=cntb[:, bass.ds(c * 7 + (k + 1), 1)])\
                        .then_inc(s_dv, 1)
                    v.wait_ge(s_dv, c * 7 + (dv + k + 1))
            dv += TILES - 1
            v.nop().then_inc(s_float, 1)
            step(v.tensor_scalar(e_rec[:, :], e_dst[:, :], DST_SHIFT, None, ALU.logical_shift_left))
            step(v.tensor_scalar(e_rel[:, :], e_rel[:, :], REL_SHIFT, None, ALU.logical_shift_left))
            own()
            step(v.tensor_tensor(e_rec[:, :], e_rec[:, :], e_rel[:, :], ALU.bitwise_or))
            own()
            v.tensor_tensor(e_rec[:, :], e_rec[:, :], e_src[:, :], ALU.bitwise_or).then_inc(s_rec, 1)

            v.wait_ge(s_pe, 1)
            step(v.tensor_copy(tl[:, 0:2], pA[0:TILES, 0:2]))
            own()
            step(v.tensor_tensor(tl[:, 2:3], tl[:, 1:2], tl[:, 0:1], ALU.subtract))
            own()
            step(v.tensor_scalar(tli[:, 0:1], tl[:, 2:3], float(P - 1), None, ALU.add))
            own()
            step(v.tensor_scalar(tli[:, 0:1], tli[:, 0:1], 7, None, ALU.arith_shift_right))
            own()
            v.tensor_scalar(tl[:, 3:4], tli[:, 0:1], 1.0, None, ALU.max).then_inc(s_chunks, 1)
            v.wait_ge(s_pe, 2)
            step(v.tensor_copy(tl[:, 4:5], pA[0:TILES, 4:5]))
            own()
            step(v.tensor_tensor(tl[:, 5:6], tl[:, 4:5], tl[:, 3:4], ALU.add))
            step(v.scalar_tensor_tensor(vals[:, 1:2], tl[:, 4:5], -float(P), tl[:, 0:1], ALU.mult, ALU.add))
            step(v.tensor_copy(vals[:, 0:1], tile_p[:, 0:1]))
            step(v.tensor_copy(vals[:, 2:3], tl[:, 1:2]))
            step(v.tensor_scalar(first[:, :], chunk_iota[:, :], tl[:, 4:5], None, ALU.is_equal))
            own()
            step(v.tensor_tensor(tl[:, 6:7], tl[:, 5:6], tile_p[:, 2:3], ALU.is_gt))
            step(v.tensor_scalar(belong[:, :], chunk_iota[:, :], tl[:, 5:6], None, ALU.is_lt))
            own()
            v.scalar_tensor_tensor(belong[:, :], chunk_iota[:, :], tl[:, 4:5], belong[:, :],
                                   ALU.is_ge, ALU.mult).then_inc(s_chunks, 1)
            v.wait_ge(s_pe, 3)
            step(v.tensor_copy(info[:, :, :], pA[:, 0:3 * BLOCKS].rearrange("p (j c) -> p j c", c=3)))
            step(v.tensor_scalar(flags[0:1, 1:2], pA[0:1, 32:33], 0.0, None, ALU.is_gt))
            step(v.tensor_copy(flagf[0:1, 0:2], pA[0:1, 34:36]))
            own()
            step(v.tensor_tensor(flagf[0:1, 2:3], flagf[0:1, 0:1], flagf[0:1, 1:2], ALU.add))
            step(v.tensor_tensor(info[:, :, 1], info[:, :, 1], chunk_start[:, :], ALU.add))
            own()
            v.tensor_scalar(flags[0:1, 0:1], flagf[0:1, 2:3], 0.0, None, ALU.is_gt).then_inc(s_dv, 1)
            dv += 1
            step(v.tensor_tensor(info[:, :, 2], info[:, :, 2], info[:, :, 1], ALU.subtract))
            step(v.tensor_scalar(run_start[:, :], info[:, :, 1], float(E), None, ALU.min))
            own()
            v.nop().then_inc(s_flags, 1)
            for h in range(2):
                step(v.tensor_scalar(toff[0:1, h * CROW:(h + 1) * CROW], (pB, pC)[h][0:1, 0:CROW],
                                     float(TILES * W), None, ALU.add))
                step(v.tensor_scalar(keep[:, h * CROW:(h + 1) * CROW], (ps[0], ps[1])[h][:, 0:CROW], -1.0, 1.0,
                                     ALU.mult, ALU.add))
            v.wait_ge(s_bnsq, 1)
            step(v.reciprocal(bn[:, 0, :], bn[:, 0, :]))
            own()
            step(v.tensor_tensor(bn[:, 1, :], bn[:, 1, :], bn[:, 0, :], ALU.mult))
            step(v.tensor_tensor(bnrow[0:1, 0, :], bnrow[0:1, 0, :], bnrow[0:1, 1, :], ALU.subtract))
            own()
            step(v.tensor_tensor(bnrow[0:1, 0, :], bnrow[0:1, 0, :], bn[0:1, 1, :], ALU.mult))
            own()
            step(v.tensor_tensor(bnrow[0:1, 0, :], bnrow[0:1, 0, :], bnrow[0:1, 2, :], ALU.add))
            for w in (wl, wr):
                for k in range(KD):
                    step(v.tensor_tensor(w[:, :, k, :], w[:, :, k, :],
                                         bn[:, 1, :].rearrange("p (l d) -> p l d", d=D), ALU.mult))
            step(v.tensor_tensor(bihc[:, 0, :], bihc[:, 0, :], bihc[:, 1, :], ALU.add))
            for q in range(TILES // XB):
                v.wait_ge(s_x[q % 2], 16 * (q // 2 + 1))
                for k in range(XB):
                    step(v.bn_stats(lns[:, k, :], xs[:, q % 2, k, :]))
                own()
                for k in range(XB):
                    i = v.bn_aggr(lnm[:, q % 2, k, 0:2], lns[:, k, :])
                i.then_inc(s_lnstat, 1)
                v.wait_ge(s_lnsq, q + 1)
                step(v.reciprocal(lnm[:, q % 2, :, 2:3], lnm[:, q % 2, :, 2:3]))
                own()
                v.scalar_tensor_tensor(lnm[:, q % 2, :, 0:1], lnm[:, q % 2, :, 0:1], -1.0,
                                       lnm[:, q % 2, :, 2:3], ALU.mult, ALU.mult).then_inc(s_lnr, 1)
            v.wait_ge(s_dv, dv)
            unsorted = v.value_load(flags[0:1, 0:1], min_val=0, max_val=1)
            late = v.value_load(flags[0:1, 1:2], min_val=0, max_val=1)
            v.wait_ge(s_lnh, TILES // XB)
            with v.If(unsorted > 0):
                v.memset(pos_f[:, :], 0.0).then_inc(s_scan, 1)
                v.tensor_tensor(ncnt[:, :], cntb[:, 1:TILES + 1], cntb[:, 0:TILES], ALU.subtract)\
                    .then_inc(s_scan, 1)
                v.tensor_scalar(diag[:, :], ident[0:TILES, 0:TILES], tl[:, 4:5], float(P), ALU.mult, ALU.mult)\
                    .then_inc(s_scan, 1)
                v.wait_ge(s_scan_pe, 1)
                v.tensor_scalar(slot0[:, :], pA[0:EP, 0:TILES], -1.0, None, ALU.add).then_inc(s_scan, 1)
                v.wait_ge(s_scan, 4)
                with v.Fori(0, TILES) as t:
                    v.tensor_scalar(e_tmp[:, :], e_f[:, :], bound[0:EP, bass.ds(t, 1)], None, ALU.is_ge)\
                        .then_inc(s_scan, 1)
                    v.wait_ge(s_scan, t * 5 + 5)
                    v.scalar_tensor_tensor(e_tmp[:, :], e_f[:, :], bound[0:EP, bass.ds(t + 1, 1)],
                                           e_tmp[:, :], ALU.is_lt, ALU.mult).then_inc(s_scan, 1)
                    v.wait_ge(s_scan, t * 5 + 6)
                    v.tensor_tensor_scan(e_scan[:, :], ones[0:EP, 0:1].to_broadcast([EP, EC]), e_tmp[:, :],
                                         slot0[:, bass.ds(t, 1)], ALU.mult, ALU.add).then_inc(s_scan, 1)
                    v.wait_ge(s_scan, t * 5 + 7)
                    v.tensor_tensor(e_scan[:, :], e_scan[:, :], e_tmp[:, :], ALU.mult).then_inc(s_scan, 1)
                    v.wait_ge(s_scan, t * 5 + 8)
                    v.tensor_tensor(pos_f[:, :], pos_f[:, :], e_scan[:, :], ALU.add).then_inc(s_scan, 1)
                    v.wait_ge(s_scan, t * 5 + 9)
                v.tensor_copy(pos_i[:, :], pos_f[:, :]).then_inc(s_pos, 1)
                v.nop().then_inc(s_posr, 1)
            v.wait_ge(s_blk, 16)
            bf = blk[:, :, :].rearrange("p j c -> p (j c)")
            step(v.tensor_scalar(u_src[:, :], bf, (1 << SRC_BITS) - 1, None, ALU.bitwise_and))
            step(v.tensor_scalar(u_dst[:, :], bf, DST_SHIFT, (1 << SRC_BITS) - 1,
                                 ALU.logical_shift_right, ALU.bitwise_and))
            step(v.tensor_scalar(u_rel[:, :], bf, REL_SHIFT, None, ALU.logical_shift_right))
            own()
            for j in range(BLOCKS):
                step(v.tensor_scalar(u_f[:, 2, j * P:(j + 1) * P], slot_iota[:, :], info[:, j, 2:3], BIG,
                                     ALU.is_ge, ALU.mult))
            step(v.scalar_tensor_tensor(u_f[:, 1, :], u_rel[:, :], float(N), u_src[:, :], ALU.mult, ALU.add))
            step(v.tensor_copy(u_f[:, 0, :], u_src[:, :]))
            own()
            for j in range(BLOCKS):
                c = slice(j * P, (j + 1) * P)
                step(v.scalar_tensor_tensor(u_f[:, 2, c], u_dst[:, c], info[:, j, 0:1], u_f[:, 2, c],
                                            ALU.subtract, ALU.add))
            own()
            v.nop().then_inc(s_unp, 1)
            n = 0
            for k, to in enumerate((idx0, idx1, dloc)):
                for h in range(2):
                    c = slice(512 * h, min(512 * (h + 1), CP))
                    v.wait_ge(s_turn, n + 1)
                    i = v.tensor_copy(to[:, c], (ps + [pA, pB])[n][:, 0:c.stop - c.start])
                    n += 1
                    i.then_inc(s_dv, 1)
                    dv += 1
            v.wait_ge(s_dv, dv)
            v.nop().then_inc(s_table, 1)
            v.nop().then_inc(s_acc0, PS)
            v.nop().then_inc(s_acc, PS)

            for L in range(LAYERS + 1):
                def offsets(i):
                    _, offs = nc.values_load_multi_w_load_instructions(
                        toff[0:1, bass.ds(i * GROUP, GROUP)], engines=(mybir.EngineType.DVE,),
                        min_val=0, max_val=TILES * W,
                        skip_runtime_bounds_check_because="the table is made of offsets of tiles")
                    return offs

                def hot(i, h, L=L):
                    v.wait_ge(s_sum, i * GROUP + (L * CHUNKS + (h + 1) * HALF))
                    v.tensor_tensor(
                        onehot[:, h * HALF:(h + 1) * HALF, :],
                        node_iota[:, :].unsqueeze(1).to_broadcast([P, HALF, TN]),
                        dloc[:, bass.ds(i * GROUP + h * HALF, HALF)].unsqueeze(2)
                        .to_broadcast([P, HALF, TN]), ALU.is_equal).then_inc(s_hot, 1)

                def add(i, u, offs, L=L):
                    v.wait_ge(s_sum, i * GROUP + (L * CHUNKS + GROUP + u + 1))
                    for s_part, c0, c1 in ((s_acc0, 0, P), (s_acc, P, W)):
                        v.wait_ge(s_part, i * GROUP + (L * CHUNKS + PS + u))
                        a = acc[0:TN, bass.ds(offs[u] + c0, c1 - c0)]
                        v.scalar_tensor_tensor(a, a, keep[0:TN, bass.ds(i * GROUP + u, 1)],
                                               ps[u % PS][0:TN, c0:c1], ALU.mult, ALU.add)\
                            .then_inc(s_part, 1)

                def group(i, todo, L=L):
                    offs = offsets(i)
                    for u in range(GROUP):
                        add(i, u, offs)
                        if u == HOT_AT[0]:
                            hot(i, 1)
                        if u == HOT_AT[1]:
                            hot(i + 1, 0)
                        if todo and u in DVE_AT[L]:
                            todo[DVE_AT[L].index(u)]()

                if L > 0:
                    v.wait_ge(s_hot, L * (2 * GROUPS + 1))
                v.wait_ge(s_sum, L * CHUNKS + GROUP)
                hot(0, 0)
                for i in range(LEAD):
                    group(i, None)
                with v.Fori(0, TILES) as t:
                    v.wait_ge(s_acc0, t * GROUP + (LEAD * GROUP + L * CHUNKS + PS))
                    v.wait_ge(s_acc, t * GROUP + (LEAD * GROUP + L * CHUNKS + PS))
                    group(t + LEAD, dve_stages(v, L, t, S_IN))
                with v.If(late > 0):
                    v.wait_ge(s_acc0, (L + 1) * CHUNKS + PS)
                    v.wait_ge(s_acc, (L + 1) * CHUNKS + PS)
                    with v.Fori(0, TILES) as t:
                        for s in dve_stages(v, L, t, S_LATE):
                            s()

        @block.tensor
        def _(pe):
            pe.wait_ge(s_float, 2)
            pe.matmul(pA[0:TILES, 0:1], cntb[:, 0:TILES], ones[0:EP, 0:1], start=True, stop=True)
            pe.matmul(pA[0:TILES, 1:2], cntb[:, 1:TILES + 1], ones[0:EP, 0:1], start=True, stop=True)\
                .then_inc(s_pe, 1)
            pe.wait_ge(s_chunks, 1)
            pe.matmul(pA[0:TILES, 4:5], tri[0:TILES, 0:TILES], tl[:, 3:4], start=True, stop=True)\
                .then_inc(s_pe, 1)
            pe.wait_ge(s_chunks, 2)
            for j in range(BLOCKS):
                pe.matmul(pA[:, 3 * j:3 * j + 3], belong[:, j * P:(j + 1) * P], vals[:, :],
                          start=True, stop=True)
            pe.matmul(pA[:, 32:33], ones[0:TILES, :], tl[:, 6:7], start=True, stop=True)
            pe.matmul(pA[:, 34:36], ones[0:EP, :], bad[:, 0:2], start=True, stop=True)
            for h in range(2):
                c = slice(h * CROW, (h + 1) * CROW)
                pe.matmul((pB, pC)[h][0:1, 0:CROW], tile_p[:, 1:2], belong[:, c], start=True, stop=True)
                i = pe.matmul(ps[h][:, 0:CROW], ones[0:TILES, :], first[:, c], start=True, stop=True)
            i.then_inc(s_pe, 1)
            pe.wait_ge(s_flags, 1)
            unsorted = pe.value_load(flags[0:1, 0:1], min_val=0, max_val=1)
            late = pe.value_load(flags[0:1, 1:2], min_val=0, max_val=1)
            with pe.If(unsorted > 0):
                pe.wait_ge(s_scan, 3)
                pe.matmul(pA[0:EP, 0:TILES], tri[0:EP, 0:EP], ncnt[:, :], start=True, stop=False)
                pe.matmul(pA[0:EP, 0:TILES], ones[0:TILES, 0:EP], diag[:, :], start=False, stop=True)\
                    .then_inc(s_scan_pe, 1)
            pe.wait_ge(s_wts, 16 * N_WTS)
            pe.wait_ge(s_unp, 1)
            n = 0
            for k in range(3):
                for h in range(2):
                    c0, c1 = 512 * h, min(512 * (h + 1), CP)
                    for c in range(c0, c1, P):
                        i = pe.transpose((ps + [pA, pB])[n][:, c - c0:c - c0 + P], u_f[:, k, c:c + P],
                                         ident[:, :])
                    i.then_inc(s_turn, 1)
                    n += 1
            pe.wait_ge(s_table, 1)
            for L in range(LAYERS + 1):
                def product(i, u, L=L):
                    if u % HALF == 0:
                        pe.wait_ge(s_hot, i * 2 + (L * (2 * GROUPS + 1) + u // HALF + 1))
                    pe.wait_ge(s_rows[u], i * 16 + 16 * (L * GROUPS + 1))
                    pe.wait_ge(s_acc, i * GROUP + (L * CHUNKS + u + 1))
                    pe.matmul(ps[u % PS][0:TN, 0:W], onehot[:, u, :], rows[:, u, :], start=True, stop=True)\
                        .then_inc(s_sum, 1)

                with pe.Fori(0, LEAD) as i:
                    for u in range(GROUP):
                        product(i, u)
                with pe.Fori(0, TILES) as t:
                    todo = pe_stages(pe, L, t, S_IN)
                    for u in range(GROUP):
                        product(t + LEAD, u)
                        if u in PE_AT[L]:
                            todo[PE_AT[L].index(u)]()
                with pe.If(late > 0):
                    with pe.Fori(0, TILES) as t:
                        for s in pe_stages(pe, L, t, S_LATE):
                            s()


_NAMES = ["x", "src", "dst", "edge_type_2", "L0_gnn_mask_embed", "L0_gnn_Wl", "L0_gnn_Wr", "L0_gnn_b",
          "L0_gnn_gamma", "L0_gnn_beta", "L0_gnn_rmean", "L0_gnn_rvar", "L1_gnn_W_rel", "L1_gnn_b_rel",
          "L1_gnn_W_ih", "L1_gnn_b_ih", "L1_gnn_b_hh", "L1_gnn_W1", "L1_gnn_b1", "L1_gnn_W2", "L1_gnn_b2",
          "L1_gnn_W3", "L1_gnn_b3"]
_TURNED = ("L1_gnn_W_rel", "L1_gnn_W_ih", "L1_gnn_W1", "L1_gnn_W2", "L1_gnn_W3")


def kernel(**inputs):
    import numpy as _np
    import concourse.bacc as _bacc
    from concourse import mybir as _mybir
    from concourse.bass_utils import run_bass_kernel_spmd as _run

    nc = _bacc.Bacc("TRN2", target_bir_lowering=False, num_devices=1)
    arrays, args = {}, []
    for name in _NAMES:
        a = _np.asarray(inputs[name])
        if name in _TURNED:
            a = _np.swapaxes(a, -1, -2)
        a = _np.ascontiguousarray(a)
        arrays[f"in_{name}_dram"] = a
        args.append(nc.dram_tensor(f"in_{name}_dram", a.shape, _mybir.dt.from_np(a.dtype),
                                   kind="ExternalInput").ap())
    args.append(nc.dram_tensor("out_0_dram", (N, D), _mybir.dt.float32, kind="ExternalOutput").ap())
    gnn(nc, *args)
    r = _run(nc, [arrays], core_ids=[0])
    return r.results[0]["out_0_dram"]
```

```python
from contextlib import ExitStack

import concourse.bass as bass
from concourse import mybir

F32 = mybir.dt.float32
I32 = mybir.dt.int32
ALU = mybir.AluOpType
ACT = mybir.ActivationFunctionType

N, E, D = 6250, 100000, 256
P = 128
KD = D // P
TN = 125
TILES = N // TN
EP, EC = 125, E // 125
GROUP = 16
HALF = GROUP // 2
CHUNKS = -(-(E // P + TILES) // GROUP) * GROUP
GROUPS = CHUNKS // GROUP
BLOCKS = -(-CHUNKS // P)
CP = BLOCKS * P
LEAD = GROUPS - TILES
W = D + 1
CROW = CP // 2
STAGED = 2 * (GROUPS + 1)
PS = 4
LAYERS = 3
EPS = 1e-5
SRC_BITS = 13
DST_SHIFT, REL_SHIFT = SRC_BITS, 2 * SRC_BITS
EMPTY = float(1 << 20)
XB = 5
STEPS = TILES // XB
COUNTS = 7
COUNTS_V = 21
assert TN * TILES == N and EP * EC == E and CHUNKS * P >= E + TILES * P and LEAD >= 2
PE_AT = [(4, 6), (2, 4), (1, 2, 3, 7, 10), (2, 4, 12, 13, 14)]
DVE_AT = [(0, 1, 2, 8), (0, 7), (0, 1, 8, 9, 10, 12, 13), (0, 9, 10, 15)]
PE_TWO = (0, 1, 2, 4, 9, 12, 13)
DVE_TWO = (0, 1, 6, 7, 8, 9, 10)
BN_AT = (0, 2, 5, 7, 9, 11)
HOT_AT = (3, 12)


def gnn(nc, x, src, dst, rel, mask_embed, Wl, Wr, b, gamma, beta, rmean, rvar,
        WrelT, b_rel, WihT, b_ih, b_hh, W1T, b1, W2T, b2, W3T, b3, out):
    ctx = ExitStack()
    with ctx:
        ctx.enter_context(nc.allow_non_contiguous_dma(reason="bias columns and row ends: a few elements"))

        def sb(name, shape, dt=F32):
            return ctx.enter_context(nc.sbuf_tensor(name, shape, dt))

        def sem(name):
            return ctx.enter_context(nc.semaphore(name))

        rec_dram = nc.dram_tensor("rec_dram", (E + P,), I32, kind="Internal").ap()
        slot_dram = nc.dram_tensor("slot_dram", (CP * P,), I32, kind="Internal").ap()
        H = [nc.dram_tensor(f"h{i}_dram", (N, D), F32, kind="Internal").ap() for i in range(LAYERS)]
        X1 = nc.dram_tensor("x1_dram", (N, D), F32, kind="Internal").ap()
        MSG = nc.dram_tensor("msg_dram", (2 * N, D), F32, kind="Internal").ap()

        ident = sb("ident", [P, P])
        ones = sb("ones", [P, P])
        tri = sb("tri", [P, P])
        node_iota = sb("node_iota", [P, TN])
        slot_iota = sb("slot_iota", [P, P])
        chunk_iota = sb("chunk_iota", [TILES, CP])
        chunk_start = sb("chunk_start", [P, BLOCKS])
        bound = sb("bound", [P, TILES + 1])
        bound_a = sb("bound_a", [P, TILES + 1])
        tile_p = sb("tile_p", [TILES, 3])
        eps_col = sb("eps_col", [P, 1])
        wl = sb("wl", [P, LAYERS, KD, D])
        wr = sb("wr", [P, LAYERS, KD, D])
        bn = sb("bn", [P, 2, LAYERS * D])
        bnrow = sb("bnrow", [1, 3, LAYERS * D])
        wrel = sb("wrel", [P, 2, KD, D])
        brelc = sb("brelc", [P, 2, KD])
        brelr = sb("brelr", [1, 2, D])
        wih = sb("wih", [P, KD, 4 * D])
        bihc = sb("bihc", [P, 2, 8])
        w1 = sb("w1", [P, KD, P])
        w2 = sb("w2", [P, P])
        w3 = sb("w3", [P, D])
        b12 = sb("b12", [P, 2])
        b3r = sb("b3r", [1, D])
        idx0 = sb("idx0", [P, CP], I32)
        idx1 = sb("idx1", [P, CP], I32)
        dloc = sb("dloc", [P, CP])
        keep = sb("keep", [P, CP])
        toff = sb("toff", [1, CP], I32)
        flags = sb("flags", [1, 2], I32)
        acc = sb("acc", [P, (TILES + 1) * W])
        rows = sb("rows", [P, GROUP, W])
        onehot = sb("onehot", [P, GROUP, TN])
        idx_st = sb("idx_st", [P, GROUP], I32)
        deg = sb("deg", [P, 1])
        rdeg = sb("rdeg", [P, TILES])
        aggn = sb("aggn", [P, D])
        ht = sb("ht", [P, D])
        xt = sb("xt", [P, D])
        tT = sb("tT", [P, 4, TN])
        hn = sb("hn", [P, D])
        x1t = sb("x1t", [P, D])
        stat = sb("stat", [P, 12])
        y1 = sb("y1", [P, 4, TN])
        msg = sb("msg", [P, 2, D])
        gate = sb("gate", [P, 6, TN])
        cell = sb("cell", [P, 2, 2, TN])
        z12 = sb("z12", [P, 2, TN])

        e_dst = sb("e_dst", [EP, EC], I32)
        e_src = sb("e_src", [EP, EC], I32)
        e_rel = sb("e_rel", [EP, EC], I32)
        e_rec = sb("e_rec", [EP, EC], I32)
        e_f = sb("e_f", [EP, EC])
        e_next = sb("e_next", [EP, 1], I32)
        e_nextf = sb("e_nextf", [EP, 1])
        bad = sb("bad", [EP, 3])
        cntb = sb("cntb", [EP, TILES + 1])
        zero_i = sb("zero_i", [P, P], I32)
        tl = sb("tl", [TILES, 8])
        tli = sb("tli", [TILES, 1], I32)
        vals = sb("vals", [TILES, 3])
        info = sb("info", [P, BLOCKS, 3])
        run_start = sb("run_start", [P, BLOCKS], I32)
        flagf = sb("flagf", [1, 3])
        blk = sb("blk", [P, BLOCKS, P], I32)
        lns = sb("lns", [TN, TILES, 6])
        lnm = sb("lnm", [TN, TILES, 3])
        e_tmp = sb("e_tmp", [EP, EC])
        st_pos = sb("st_pos", [EP, 8], I32)
        st_rec = sb("st_rec", [EP, 8], I32)
        ncnt = sb("ncnt", [EP, TILES])
        diag = sb("diag", [TILES, TILES])
        slot0 = sb("slot0", [EP, TILES])
        xs = acc[0:TN, 0:TILES * D].rearrange("p (t d) -> p t d", d=D)
        rows_flat = rows[:, :, :].rearrange("p g w -> p (g w)")
        u_idx = rows_flat[:, 0:CP]
        e_scan = rows_flat[0:EP, CP:CP + EC]
        tab = sb("tab", [P, 2, CP])
        belong = tab[0:TILES, 0, :]
        first = tab[0:TILES, 1, :]
        pos_f = tab[0:EP, 0, 0:EC]
        pos_i = tab[0:EP, 1, 0:EC].bitcast(I32)
        u_node = tab[:, 0, :]
        u_msg = tab[:, 1, :]
        u_rec = blk[:, :, :].rearrange("p j c -> p (j c)")
        below_v = (e_tmp[:, :], e_scan)
        below_a = (tab[0:EP, 0, 0:EC], tab[0:EP, 1, 0:EC])
        hot_i = onehot[:, :, :].rearrange("p a b -> p (a b)").bitcast(I32)
        u_src = hot_i[:, 0:CP]
        u_dst = hot_i[:, CP:2 * CP]

        weights = []
        lay = "l (k p) n -> p l k n"
        weights.append((bn[:, 0, :], rvar.rearrange("l d -> (l d)").partition_broadcast(P)))
        weights.append((bn[:, 1, :], gamma.rearrange("l d -> (l d)").partition_broadcast(P)))
        for k, w in enumerate((b, rmean, beta)):
            weights.append((bnrow[0:1, k, :], w.rearrange("(a l) d -> a (l d)", a=1)))
        weights.append((wl[:, :, :, :], Wl.rearrange(lay, p=P)))
        weights.append((wr[:, :, :, :], Wr.rearrange(lay, p=P)))
        weights.append((wrel[:, :, :, :], WrelT.rearrange(lay, p=P)))
        weights.append((brelc[:, :, :], b_rel.rearrange("r (k p) -> p r k", p=P)))
        weights.append((brelr[:, :, :], b_rel.rearrange("(a r) d -> a r d", a=1)))
        weights.append((wih[:, :, :], WihT.rearrange("(k p) n -> p k n", p=P)))
        weights.append((bihc[:, 0, :], b_ih.rearrange("(c p) -> p c", p=P)))
        weights.append((bihc[:, 1, :], b_hh.rearrange("(c p) -> p c", p=P)))
        weights.append((w1[:, :, :], W1T.rearrange("(k p) n -> p k n", p=P)))
        weights.append((w2[:, :], W2T))
        weights.append((w3[:, :], W3T))
        weights.append((b12[:, 0:1], b1.rearrange("(p a) -> p a", a=1)))
        weights.append((b12[:, 1:2], b2.rearrange("(p a) -> p a", a=1)))
        weights.append((b3r[0:1, :], b3.rearrange("(a d) -> a d", a=1)))
        N_WTS = len(weights)
        N_CONST = 15

        def bank(name):
            return ctx.enter_context(nc.psum_tensor(name, [P, 512], F32))

        ps = [bank(f"ps{i}") for i in range(PS)]
        pA, pB, pC, pD = bank("pA"), bank("pB"), bank("pC"), bank("pD")

        s_const = sem("s_const")
        s_wts = sem("s_wts")
        s_edges = sem("s_edges")
        s_float = sem("s_float")
        s_rec = sem("s_rec")
        s_rec_out = sem("s_rec_out")
        s_dv = sem("s_dv")
        s_pe = sem("s_pe")
        s_blk = sem("s_blk")
        s_flags = sem("s_flags")
        s_fill = sem("s_fill")
        s_posr = sem("s_posr")
        s_stage = sem("s_stage")
        s_scat = sem("s_scat")
        s_scat_all = sem("s_scat_all")
        s_pos = sem("s_pos")
        s_run = sem("s_run")
        s_chunks = sem("s_chunks")
        s_scan = sem("s_scan")
        s_scan_pe = sem("s_scan_pe")
        s_unp = sem("s_unp")
        s_turn = sem("s_turn")
        s_x = [sem(f"s_x{q}") for q in range(STEPS)]
        s_lnstat = sem("s_lnstat")
        s_lnsq = sem("s_lnsq")
        s_lnr = sem("s_lnr")
        s_lnh = sem("s_lnh")
        s_h0 = [sem("s_h0_first"), sem("s_h0_rest")]
        s_cnt_v = sem("s_cnt_v")
        s_cnt_a = sem("s_cnt_a")
        s_counted = sem("s_counted")
        s_mask = sem("s_mask")
        s_bnsq = sem("s_bnsq")
        s_idx0 = sem("s_idx0")
        s_idx1 = sem("s_idx1")
        s_bnready = sem("s_bnready")
        s_held_v = sem("s_held_v")
        s_held_s = sem("s_held_s")
        s_held_g = sem("s_held_g")
        s_idx = sem("s_idx")
        s_rows = [sem(f"s_rows{u}") for u in range(GROUP)]
        s_rows_last = [sem(f"s_rows_last{u}") for u in range(GROUP)]
        s_hot = sem("s_hot")
        s_sum = sem("s_sum")
        s_acc0 = sem("s_acc0")
        s_acc = sem("s_acc")

        def dense_sems(n):
            names = ("loaded", "xloaded", "deg", "res", "scaled", "tr", "trc", "z", "new", "stored", "stored2",
                     "msgfree", "var", "sd", "rstd", "norm", "trh", "trhc", "y1", "y1c", "y2", "y2c",
                     "gates", "gatec", "cell", "cellt", "hid", "w1", "w1c", "w2", "w2c")
            return {k: sem(f"s_{n}_{k}") for k in names}

        S = dense_sems("dense")

        block = ctx.enter_context(nc.Block())

        BASE = {L: L * TILES for L in range(LAYERS + 1)}

        def tile_rows(t):
            return bass.ds(t * TN, TN)

        def sp_load(sp, L, t, S):
            if L < LAYERS:
                sp.dma_start(ht[0:TN, :], H[L][tile_rows(t), :]).then_inc(S["loaded"], 16)
            else:
                sp.dma_start(xt[0:TN, :], X1[tile_rows(t), :]).then_inc(S["loaded"], 16)
            if L == LAYERS - 1:
                sp.dma_start(xt[0:TN, :], x[tile_rows(t), :]).then_inc(S["xloaded"], 16)

        def sp_store(sp, L, t, S, more):
            n = BASE[L]
            sp.wait_ge(S["new"], t + (n + 1))
            if L == LAYERS - 1:
                sp.dma_start(X1[tile_rows(t), :], x1t[0:TN, :]).then_inc(S["stored"], 16)
                if more:
                    sp_load(sp, L, t + 1, S)
                sp.wait_ge(S["y2c"], t + 1)
                sp.dma_start(MSG.rearrange("(r n) d -> n r d", r=2)[tile_rows(t), :, :],
                             msg[0:TN, :, :]).then_inc(S["stored2"], 16)
                sp.wait_ge(S["stored2"], t * 16 + 16)
                sp.sem_inc(S["msgfree"], 1)
            else:
                to = H[L + 1] if L < LAYERS - 1 else out
                sp.dma_start(to[tile_rows(t), :], hn[0:TN, :]).then_inc(S["stored"], 16)
                sp.wait_ge(S["stored"], t * 16 + 16 * (n + 1))
                sp.sem_inc(s_held_s, 1)
                if more:
                    sp_load(sp, L, t + 1, S)

        def sp_dense(sp, L, S):
            sp_load(sp, L, 0, S)
            if L == LAYERS - 1:
                sp.sem_inc(S["msgfree"], 1)
            with sp.Fori(0, TILES - 1) as t:
                sp_store(sp, L, t, S, True)
            sp_store(sp, L, TILES - 1, S, False)

        def dve_stages(v, L, t, S):
            n = BASE[L]
            a = acc[0:TN, bass.ds(t * W, D)]
            inv = rdeg[0:TN, bass.ds(t, 1)]

            def degree():
                v.tensor_scalar(deg[0:TN, :], acc[0:TN, bass.ds(t * W + D, 1)], 1.0, None, ALU.max)\
                    .then_inc(S["deg"], 1)

            def inverse():
                v.wait_ge(S["deg"], t * 2 + 1)
                v.reciprocal(inv, deg[0:TN, :]).then_inc(S["deg"], 1)

            def scale():
                if L == 0:
                    v.wait_ge(S["deg"], t * 2 + 2)
                if L < LAYERS:
                    v.tensor_scalar(aggn[0:TN, :], a, inv, None, ALU.mult).then_inc(S["scaled"], 1)
                else:
                    v.tensor_copy(aggn[0:TN, :], a).then_inc(S["scaled"], 1)

            def old():
                v.wait_ge(S["loaded"], t * 16 + 16 * (n + 1))
                v.wait_ge(S["xloaded"], t * 16 + 16)
                v.tensor_tensor(xt[0:TN, :], ht[0:TN, :], xt[0:TN, :], ALU.add).then_inc(S["res"], 1)

            def new():
                v.wait_ge(S["z"], t + (n + 1))
                if L < LAYERS - 1:
                    v.wait_ge(S["loaded"], t * 16 + 16 * (n + 1))
                    v.scalar_tensor_tensor(hn[0:TN, :], pB[0:TN, 0:D], 0.0, ht[0:TN, :], ALU.max, ALU.add)\
                        .then_inc(S["new"], 1)
                elif L == LAYERS - 1:
                    v.wait_ge(S["res"], t + 1)
                    v.wait_ge(S["stored"], t * 16 + 16 * n)
                    v.tensor_tensor(x1t[0:TN, :], pB[0:TN, 0:D], xt[0:TN, :], ALU.add)\
                        .then_inc(S["new"], 1)
                else:
                    v.wait_ge(S["loaded"], t * 16 + 16 * (n + 1))
                    v.tensor_tensor(hn[0:TN, :], pB[0:TN, 0:D], xt[0:TN, :], ALU.add)\
                        .then_inc(S["new"], 1)

            def stats():
                v.wait_ge(S["new"], t + (n + 1))
                v.bn_stats(stat[0:TN, 0:6], x1t[0:TN, :]).then_inc(S["var"], 1)

            def variance():
                v.wait_ge(S["var"], t * 2 + 1)
                v.sem_inc(s_held_v, 1)
                v.bn_aggr(stat[0:TN, 6:8], stat[0:TN, 0:6]).then_inc(S["var"], 1)

            def rstd():
                v.wait_ge(S["sd"], t + 1)
                v.reciprocal(stat[0:TN, 9:10], stat[0:TN, 8:9]).then_inc(S["rstd"], 1)

            def norm():
                v.wait_ge(S["rstd"], t + 1)
                v.tensor_scalar(hn[0:TN, :], x1t[0:TN, :], stat[0:TN, 6:7], stat[0:TN, 9:10],
                                ALU.subtract, ALU.mult).then_inc(S["norm"], 1)

            def cells():
                v.wait_ge(S["gatec"], t + 1)
                v.tensor_tensor(cell[:, 0, :, :], gate[:, 0:2, :], gate[:, 2:4, :], ALU.mult)\
                    .then_inc(S["cell"], 1)

            def hidden():
                v.wait_ge(S["cellt"], t + 1)
                v.tensor_tensor(cell[:, 0, :, :], gate[:, 4:6, :], cell[:, 1, :, :], ALU.mult)\
                    .then_inc(S["hid"], 1)

            if L == 0:
                return [degree, inverse, scale, new]
            if L < LAYERS - 1:
                return [scale, new]
            if L == LAYERS - 1:
                return [scale, old, new, stats, variance, rstd, norm]
            return [scale, cells, hidden, new]

        def act_turned(a, L, t, S):
            a.wait_ge(S["tr"], t + (BASE[L] + 1))
            k = 4 if L < LAYERS else 2
            a.copy(tT[:, 0:k, :], pA[:, 0:k * TN].rearrange("p (k n) -> p k n", k=k)).then_inc(S["trc"], 1)

        def act_sd(a, t, S):
            a.wait_ge(S["var"], t * 2 + 2)
            a.activation(stat[0:TN, 8:9], stat[0:TN, 7:8], ACT.Sqrt, bias=eps_col[0:TN, :])\
                .then_inc(S["sd"], 1)

        def act_turned_h(a, t, S):
            a.wait_ge(S["trh"], t + 1)
            a.activation(tT[:, 0:2, :], pA[:, 0:2 * TN].rearrange("p (k n) -> p k n", k=2), ACT.Relu)\
                .then_inc(S["trhc"], 1)

        def act_y1(a, t, S):
            a.wait_ge(S["y1"], t + 1)
            for q in range(4):
                i = a.activation(y1[:, q, :], pC[:, q * TN:(q + 1) * TN], ACT.Relu,
                                 bias=brelc[:, q // 2, q % 2:q % 2 + 1])
            i.then_inc(S["y1c"], 1)

        def act_y2(a, t, S):
            a.wait_ge(S["msgfree"], t + 1)
            a.wait_ge(S["y2"], t + 1)
            a.activation(msg[0:TN, :, :], pD[0:TN, :].rearrange("p (r d) -> p r d", r=2), ACT.Relu)\
                .then_inc(S["y2c"], 1)

        def act_gates(a, t, S):
            a.wait_ge(S["gates"], t + 1)
            for q, (c, f) in enumerate(((0, ACT.Sigmoid), (1, ACT.Sigmoid), (4, ACT.Tanh),
                                        (5, ACT.Tanh), (6, ACT.Sigmoid), (7, ACT.Sigmoid))):
                p = pB[:, q * TN:(q + 1) * TN] if q < 4 else pC[:, (q - 4) * TN:(q - 3) * TN]
                i = a.activation(gate[:, q, :], p, f, bias=bihc[:, 0, c:c + 1])
            i.then_inc(S["gatec"], 1)
            a.wait_ge(S["cell"], t + 1)
            a.activation(cell[:, 1, :, :], cell[:, 0, :, :], ACT.Tanh).then_inc(S["cellt"], 1)

        def act_mlp(a, t, S, k):
            a.wait_ge(S[f"w{k}"], t + 1)
            a.activation(z12[:, k - 1, :], pD[:, (k - 1) * P:(k - 1) * P + TN], ACT.Relu,
                         bias=b12[:, k - 1:k]).then_inc(S[f"w{k}c"], 1)

        def pe_turn(pe, L, t, S):
            n = BASE[L]
            pe.wait_ge(S["scaled"], t + (n + 1))
            if L < LAYERS:
                pe.wait_ge(S["loaded"], t * 16 + 16 * (n + 1))
            for k in range(4 if L < LAYERS else 2):
                frm = aggn if k < 2 else ht
                i = pe.transpose(pA[:, k * TN:(k + 1) * TN], frm[0:TN, (k % 2) * P:(k % 2 + 1) * P],
                                 ident[0:TN, 0:TN])
            i.then_inc(S["tr"], 1)

        def pe_z(pe, L, t, S):
            pe.wait_ge(S["trc"], t + (BASE[L] + 1))
            for k in range(4):
                w = (wl if k < 2 else wr)[:, L, k % 2, :]
                pe.matmul(pB[0:TN, 0:D], tT[:, k, :], w, start=(k == 0), stop=False)
            pe.matmul(pB[0:TN, 0:D], ones[0:1, 0:TN], bnrow[0:1, 0, L * D:(L + 1) * D],
                      start=False, stop=True).then_inc(S["z"], 1)

        def pe_turn_h(pe, t, S):
            pe.wait_ge(S["norm"], t + 1)
            for k in range(2):
                i = pe.transpose(pA[:, k * TN:(k + 1) * TN], hn[0:TN, k * P:(k + 1) * P], ident[0:TN, 0:TN])
            i.then_inc(S["trh"], 1)

        def pe_y1(pe, t, S):
            pe.wait_ge(S["trhc"], t + 1)
            for q in range(4):
                r, m = q // 2, q % 2
                for k in range(2):
                    i = pe.matmul(pC[:, q * TN:(q + 1) * TN], wrel[:, r, k, m * P:(m + 1) * P],
                                  tT[:, k, :], start=(k == 0), stop=(k == 1))
            i.then_inc(S["y1"], 1)

        def pe_y2(pe, t, S):
            pe.wait_ge(S["y1c"], t + 1)
            for r in range(2):
                o = pD[0:TN, r * D:(r + 1) * D]
                for k in range(2):
                    pe.matmul(o, y1[:, 2 * r + k, :], wrel[:, r, k, :], start=(k == 0), stop=False)
                i = pe.matmul(o, ones[0:1, 0:TN], brelr[0:1, r, :], start=False, stop=True)
            i.then_inc(S["y2"], 1)

        def pe_gates(pe, t, S):
            pe.wait_ge(S["trc"], t + (BASE[LAYERS] + 1))
            for q, c in enumerate((0, 1, 4, 5, 6, 7)):
                o = pB[:, q * TN:(q + 1) * TN] if q < 4 else pC[:, (q - 4) * TN:(q - 3) * TN]
                for k in range(2):
                    i = pe.matmul(o, wih[:, k, c * P:(c + 1) * P], tT[:, k, :],
                                  start=(k == 0), stop=(k == 1))
            i.then_inc(S["gates"], 1)

        def pe_w1(pe, t, S):
            pe.wait_ge(S["hid"], t + 1)
            for k in range(2):
                i = pe.matmul(pD[:, 0:TN], w1[:, k, :], cell[:, 0, k, :], start=(k == 0), stop=(k == 1))
            i.then_inc(S["w1"], 1)

        def pe_w2(pe, t, S):
            pe.wait_ge(S["w1c"], t + 1)
            pe.matmul(pD[:, P:P + TN], w2[:, :], z12[:, 0, :], start=True, stop=True).then_inc(S["w2"], 1)

        def pe_w3(pe, t, S):
            pe.wait_ge(S["w2c"], t + 1)
            pe.matmul(pB[0:TN, 0:D], z12[:, 1, :], w3[:, :], start=True, stop=False)
            pe.matmul(pB[0:TN, 0:D], ones[0:1, 0:TN], b3r[0:1, :], start=False, stop=True)\
                .then_inc(S["z"], 1)

        def pe_stages(pe, L, t, S):
            if L < LAYERS:
                return [lambda: pe_turn(pe, L, t, S), lambda: pe_z(pe, L, t, S)]
            return [lambda: pe_turn(pe, L, t, S), lambda: pe_gates(pe, t, S),
                    lambda: pe_w1(pe, t, S), lambda: pe_w2(pe, t, S), lambda: pe_w3(pe, t, S)]

        def pe_messages(pe, t, S):
            return [lambda: pe_turn_h(pe, t, S), lambda: pe_y1(pe, t, S), lambda: pe_y2(pe, t, S)]

        @block.sync
        def _(sp):
            sp.dma_start(e_dst[:, :], dst.rearrange("(p c) -> p c", c=EC)).then_inc(s_edges, 16)
            sp.dma_start(e_next[0:EP - 1, :], dst.rearrange("(p c) -> p c", c=EC)[1:EP, 0:1])\
                .then_inc(s_edges, 16)
            sp.dma_start(e_src[:, :], src.rearrange("(p c) -> p c", c=EC)).then_inc(s_edges, 16)
            sp.dma_start(e_rel[:, :], rel.rearrange("(p c) -> p c", c=EC)).then_inc(s_edges, 16)
            xv = x.rearrange("(q t p) d -> q p t d", p=TN, t=XB)
            hv = H[0].rearrange("(q t p) d -> q p t d", p=TN, t=XB)
            for q in range(STEPS):
                sp.dma_start(xs[:, q * XB:(q + 1) * XB, :], xv[q, :, :, :]).then_inc(s_x[q], 16)
            sp.wait_ge(s_rec, 1)
            sp.dma_start(rec_dram[0:E].rearrange("(p c) -> p c", c=EC), e_rec[:, :]).then_inc(s_rec_out, 16)
            sp.wait_ge(s_const, N_CONST)
            sp.dma_start(rec_dram[E:E + P].rearrange("(a d) -> a d", a=1), zero_i[0:1, :])\
                .then_inc(s_rec_out, 16)
            for to, frm in weights:
                sp.dma_start(to, frm).then_inc(s_wts, 16)
            for q in range(STEPS):
                sp.wait_ge(s_lnh, q + 1)
                sp.dma_start(hv[q, :, :, :], xs[:, q * XB:(q + 1) * XB, :]).then_inc(s_h0[min(q, 1)], 16)
                if q == 1:
                    sp.wait_ge(s_h0[0], 16)
                    sp.dma_start(H[0][0:1, :], mask_embed.rearrange("(a d) -> a d", a=1)).then_inc(s_mask, 16)
            sp.wait_ge(s_h0[1], 16 * (STEPS - 1))
            sp.wait_ge(s_mask, 16)
            sp.wait_ge(s_rec_out, 32)
            sp.wait_ge(s_flags, 1)
            unsorted = sp.value_load(flags[0:1, 0:1], min_val=0, max_val=1)
            with sp.If(unsorted > 0):
                sv = slot_dram.rearrange("(j p c) -> j p c", p=P, c=P)
                for j in range(BLOCKS):
                    sp.dma_start(sv[j, :, :], zero_i[:, :]).then_inc(s_fill, 16)
                sp.wait_ge(s_fill, 16 * BLOCKS)
                sp.wait_ge(s_scat_all, 1)
                sp.dma_start(blk[:, :, :], slot_dram.rearrange("(j p c) -> p j c", p=P, c=P))\
                    .then_inc(s_blk, 16)
                sp.wait_ge(s_blk, 16)
            for L in range(LAYERS + 1):
                sp_dense(sp, L, S)

        @block.gpsimd
        def _(g):
            g.memset(ones[:, :], 1.0).then_inc(s_const, 1)
            g.memset(ident[:, :], 0.0).then_inc(s_const, 1)
            g.memset(eps_col[:, :], EPS).then_inc(s_const, 1)
            g.memset(zero_i[:, :], 0).then_inc(s_const, 1)
            g.wait_ge(s_const, 4)
            g.affine_select(out=ident[:, :], in_=ident[:, :], compare_op=ALU.not_equal, fill=1.0, base=0,
                            pattern=[[-1, P]], channel_multiplier=1).then_inc(s_const, 1)
            g.affine_select(out=tri[:, :], in_=ones[:, :], compare_op=ALU.is_gt, fill=0.0, base=0,
                            pattern=[[1, P]], channel_multiplier=-1).then_inc(s_const, 1)

            def iota(ap, pattern, base, cm):
                g.iota(ap, pattern=pattern, base=base, channel_multiplier=cm,
                       allow_small_or_imprecise_dtypes=True).then_inc(s_const, 1)

            iota(bound[:, :], [[TN, TILES + 1]], 0, 0)
            iota(bound_a[:, :], [[-2 * TN, TILES + 1]], 1, 0)
            iota(node_iota[:, :], [[1, TN]], 0, 0)
            iota(slot_iota[:, :], [[1, P]], 0, 0)
            iota(chunk_iota[:, :], [[1, CP]], 0, 0)
            iota(chunk_start[:, :], [[P * P, BLOCKS]], 0, P)
            iota(tile_p[:, 0:1], [[0, 1]], 0, TN)
            iota(tile_p[:, 1:2], [[0, 1]], -TILES * W, W)
            iota(tile_p[:, 2:3], [[0, 1]], GROUP * LEAD, GROUP)
            g.wait_ge(s_flags, 1)
            unsorted = g.value_load(flags[0:1, 0:1], min_val=0, max_val=1)
            late = g.value_load(flags[0:1, 1:2], min_val=0, max_val=1)
            with g.If(unsorted > 0):
                g.wait_ge(s_fill, 16 * BLOCKS)
                with g.Fori(0, EC // 8) as c:
                    g.wait_ge(s_stage, c * 2 + 2)
                    g.sem_inc(s_held_g, 1)
                    for k in range(8):
                        g.indirect_dma_start(
                            slot_dram.rearrange("(n a) -> n a", a=1),
                            bass.IndirectOffsetOnAxis(st_pos[:, k:k + 1], 0),
                            st_rec[:, k:k + 1], None).then_inc(s_scat, 16)
                    g.wait_ge(s_scat, c * 128 + 128)
                    g.nop().then_inc(s_posr, 1)
                g.nop().then_inc(s_scat_all, 1)
            with g.If(unsorted == 0):
                g.wait_ge(s_rec_out, 32)
                for j in range(BLOCKS):
                    g.indirect_dma_start(blk[:, j, :], None, rec_dram.rearrange("(n a) -> n a", a=1),
                                         bass.IndirectOffsetOnAxis(run_start[:, j:j + 1], 0))\
                        .then_inc(s_run, 16)
                g.wait_ge(s_run, 16 * BLOCKS)
                g.nop().then_inc(s_blk, 16)
            g.wait_ge(s_h0[1], 16 * (STEPS - 1))
            g.wait_ge(s_mask, 16)
            for L in range(LAYERS + 1):
                if L > 0:
                    g.wait_ge(S["stored"], 16 * BASE[L])
                    if L == LAYERS:
                        g.wait_ge(S["stored2"], 16 * TILES)
                table = H[L] if L < LAYERS else MSG

                def gathers(i, landed, L=L, table=table):
                    for u in range(GROUP):
                        if u % HALF == 0:
                            g.wait_ge(s_idx, i * 2 + (L * STAGED + u // HALF + 1))
                            g.sem_inc(s_held_g, 1)
                        g.indirect_dma_start(rows[:, u, 0:D], None, table,
                                             bass.IndirectOffsetOnAxis(idx_st[:, u:u + 1], 0))\
                            .then_inc(landed[u], 16)

                with g.Fori(0, GROUPS - 1) as i:
                    gathers(i, s_rows)
                with g.If(late > 0):
                    gathers(GROUPS - 1, s_rows_last)

        @block.scalar
        def _(a):
            a.wait_ge(s_edges, 64)
            a.copy(e_f[:, :], e_dst[:, :]).then_inc(s_float, 1)
            a.wait_ge(s_const, N_CONST)
            a.wait_ge(s_float, 1)
            a.nop().then_inc(s_cnt_a, 2)
            with a.Fori(0, (TILES - 1 - COUNTS_V) // COUNTS) as c:
                for k in range(COUNTS):
                    t = c * COUNTS + (COUNTS_V + 1 + k)
                    if COUNTS % 2 and k == 0:
                        a.wait_ge(s_cnt_a, c * COUNTS + 2)
                    else:
                        a.wait_ge(s_cnt_a, c * COUNTS + (k + 1))
                    a.activation(below_a[k % 2], e_f[:, :], ACT.Sign, bias=bound_a[0:EP, bass.ds(t, 1)],
                                 scale=2.0, accum_out=cntb[:, bass.ds(t, 1)]).then_inc(s_cnt_a, 1)
            for q in range(STEPS + 1):
                if q < STEPS:
                    t = slice(q * XB, (q + 1) * XB)
                    a.wait_ge(s_lnstat, q + 1)
                    a.activation(lnm[:, t, 2:3], lnm[:, t, 1:2], ACT.Sqrt, bias=eps_col[0:TN, :])\
                        .then_inc(s_lnsq, 1)
                if q > 0:
                    a.wait_ge(s_lnr, q)
                    for k in range((q - 1) * XB, q * XB):
                        i = a.activation(xs[:, k, :], xs[:, k, :], ACT.Relu,
                                         bias=lnm[:, k, 0:1], scale=lnm[:, k, 2:3])
                    i.then_inc(s_lnh, 1)
            a.wait_ge(s_wts, 16 * N_WTS)
            a.activation(bn[:, 0, :], bn[:, 0, :], ACT.Sqrt, bias=eps_col[:, :]).then_inc(s_bnsq, 1)
            a.wait_ge(s_flags, 1)
            unsorted = a.value_load(flags[0:1, 0:1], min_val=0, max_val=1)
            late = a.value_load(flags[0:1, 1:2], min_val=0, max_val=1)
            with a.If(unsorted > 0):
                a.wait_ge(s_pos, 1)
                with a.Fori(0, EC // 8) as c:
                    a.wait_ge(s_posr, c + 1)
                    a.copy(st_pos[:, :], pos_i[:, bass.ds(c * 8, 8)]).then_inc(s_stage, 1)
                    a.copy(st_rec[:, :], e_rec[:, bass.ds(c * 8, 8)]).then_inc(s_stage, 1)
            a.wait_ge(s_idx0, 1)

            for L in range(LAYERS + 1):
                idx = idx0 if L < LAYERS else idx1

                def stage(i, h, L=L, idx=idx):
                    a.wait_ge(s_sum, i * GROUP + (L * CHUNKS + (h + 1) * HALF))
                    a.copy(idx_st[:, h * HALF:(h + 1) * HALF],
                           idx[:, bass.ds(i * GROUP + h * HALF, HALF)]).then_inc(s_idx, 1)

                def early(t):
                    act_turned(a, L, t, S)
                    if L == LAYERS:
                        act_gates(a, t, S)

                def middle(t):
                    if L == LAYERS:
                        act_mlp(a, t, S, 1)
                        act_mlp(a, t, S, 2)

                a.wait_ge(s_sum, L * CHUNKS + GROUP)
                if L == LAYERS:
                    a.wait_ge(s_idx1, 2)
                if L > 0:
                    a.wait_ge(s_idx, L * STAGED)
                stage(0, 0)
                stage(0, 1)
                if L == 0:
                    for h in range(2):
                        c = slice(512 * h, min(512 * (h + 1), CP))
                        a.wait_ge(s_turn, 5 + h)
                        i = a.copy(idx1[:, c], (pA, pB)[h][:, 0:c.stop - c.start])
                        i.then_inc(s_idx1, 1)
                for i in range(LEAD):
                    stage(i + 1, 0)
                    stage(i + 1, 1)
                with a.If(late == 0):
                    if L == LAYERS - 1:
                        act_turned(a, L, 0, S)
                        stage(LEAD + 1, 0)
                        act_sd(a, 0, S)
                        stage(LEAD + 1, 1)
                        with a.Fori(0, TILES - 3) as t:
                            act_turned_h(a, t, S)
                            act_y1(a, t, S)
                            act_turned(a, L, t + 1, S)
                            stage(t + (LEAD + 2), 0)
                            act_y2(a, t, S)
                            act_sd(a, t + 1, S)
                            stage(t + (LEAD + 2), 1)
                        t = TILES - 3
                        act_turned_h(a, t, S)
                        act_y1(a, t, S)
                        act_turned(a, L, t + 1, S)
                        stage(t + (LEAD + 2), 0)
                        act_sd(a, t + 1, S)
                        act_y2(a, t, S)
                        act_turned_h(a, t + 1, S)
                        act_y1(a, t + 1, S)
                        stage(t + (LEAD + 2), 1)
                        t = TILES - 1
                        act_turned(a, L, t, S)
                        act_sd(a, t, S)
                        act_y2(a, t - 1, S)
                        act_turned_h(a, t, S)
                        act_y1(a, t, S)
                        act_y2(a, t, S)
                    else:
                        with a.Fori(0, TILES - 1) as t:
                            early(t)
                            stage(t + (LEAD + 1), 0)
                            middle(t)
                            stage(t + (LEAD + 1), 1)
                        early(TILES - 1)
                        middle(TILES - 1)
                    a.wait_ge(s_idx, (L + 1) * STAGED - 2)
                    a.sem_inc(s_idx, 2)
                with a.If(late > 0):
                    with a.Fori(0, TILES) as t:
                        stage(t + (LEAD + 1), 0)
                        stage(t + (LEAD + 1), 1)
                    with a.Fori(0, TILES) as t:
                        early(t)
                        middle(t)
                        if L == LAYERS - 1:
                            act_sd(a, t, S)
                            act_turned_h(a, t, S)
                            act_y1(a, t, S)
                            act_y2(a, t, S)

        @block.vector
        def _(v):
            dv = 0

            def step(i):
                nonlocal dv
                i.then_inc(s_dv, 1)
                dv += 1

            def own():
                v.wait_ge(s_dv, dv)

            v.wait_ge(s_edges, 64)
            step(v.tensor_scalar(e_rec[:, :], e_dst[:, :], DST_SHIFT, None, ALU.logical_shift_left))
            step(v.tensor_scalar(e_rel[:, :], e_rel[:, :], REL_SHIFT, None, ALU.logical_shift_left))
            own()
            step(v.tensor_tensor(e_rec[:, :], e_rec[:, :], e_rel[:, :], ALU.bitwise_or))
            own()
            v.tensor_tensor(e_rec[:, :], e_rec[:, :], e_src[:, :], ALU.bitwise_or).then_inc(s_rec, 1)
            step(v.memset(cntb[:, 0:1], 0.0))
            step(v.memset(cntb[:, TILES:TILES + 1], float(EC)))
            step(v.memset(acc[0:TN, TILES * D:], 0.0))
            v.wait_ge(s_float, 1)
            step(v.scalar_tensor_tensor(e_tmp[:, 0:EC - 1], e_f[:, 0:EC - 1], 1.0, e_f[:, 1:EC],
                                        ALU.mult, ALU.is_gt, accum_out=bad[:, 0:1]))
            step(v.tensor_copy(bad[:, 2:3], e_f[:, EC - 1:EC]))
            step(v.memset(bad[:, 1:2], 0.0))
            step(v.tensor_copy(e_nextf[0:EP - 1, :], e_next[0:EP - 1, :]))
            own()
            step(v.tensor_tensor(bad[0:EP - 1, 1:2], bad[0:EP - 1, 2:3], e_nextf[0:EP - 1, :], ALU.is_gt))
            v.wait_ge(s_const, N_CONST)
            v.nop().then_inc(s_cnt_v, 2)
            with v.Fori(0, COUNTS_V // COUNTS) as c:
                for k in range(COUNTS):
                    t = c * COUNTS + (k + 1)
                    if COUNTS % 2 and k == 0:
                        v.wait_ge(s_cnt_v, c * COUNTS + 2)
                    else:
                        v.wait_ge(s_cnt_v, c * COUNTS + (k + 1))
                    v.tensor_scalar(below_v[k % 2], e_f[:, :], bound[0:EP, bass.ds(t, 1)], 0.0,
                                    ALU.is_lt, ALU.add, accum_out=cntb[:, bass.ds(t, 1)])\
                        .then_inc(s_cnt_v, 1)

            def norm_stats(q):
                v.wait_ge(s_x[q], 16)
                for t in range(q * XB, (q + 1) * XB):
                    step(v.bn_stats(lns[:, t, :], xs[:, t, :]))
                own()
                for t in range(q * XB, (q + 1) * XB):
                    i = v.bn_aggr(lnm[:, t, 0:2], lns[:, t, :])
                i.then_inc(s_lnstat, 1)

            def norm_scales(q):
                t = slice(q * XB, (q + 1) * XB)
                v.wait_ge(s_lnsq, q + 1)
                step(v.reciprocal(lnm[:, t, 2:3], lnm[:, t, 2:3]))
                own()
                v.scalar_tensor_tensor(lnm[:, t, 0:1], lnm[:, t, 0:1], -1.0, lnm[:, t, 2:3],
                                       ALU.mult, ALU.mult).then_inc(s_lnr, 1)

            norm_stats(0)
            v.wait_ge(s_cnt_v, COUNTS_V + 2)
            v.wait_ge(s_cnt_a, TILES - 1 - COUNTS_V + 2)
            v.tensor_scalar(cntb[:, COUNTS_V + 1:TILES], cntb[:, COUNTS_V + 1:TILES], -0.5, EC / 2,
                            ALU.mult, ALU.add).then_inc(s_counted, 1)
            norm_stats(1)

            v.wait_ge(s_pe, 1)
            step(v.tensor_copy(tl[:, 0:2], pA[0:TILES, 0:2]))
            own()
            step(v.tensor_tensor(tl[:, 2:3], tl[:, 1:2], tl[:, 0:1], ALU.subtract))
            own()
            step(v.tensor_scalar(tli[:, 0:1], tl[:, 2:3], float(P - 1), None, ALU.add))
            own()
            step(v.tensor_scalar(tli[:, 0:1], tli[:, 0:1], 7, None, ALU.arith_shift_right))
            own()
            v.tensor_scalar(tl[:, 3:4], tli[:, 0:1], 1.0, None, ALU.max).then_inc(s_chunks, 1)
            norm_scales(0)
            v.wait_ge(s_pe, 2)
            step(v.tensor_copy(tl[:, 4:5], pA[0:TILES, 4:5]))
            own()
            step(v.tensor_tensor(tl[:, 5:6], tl[:, 4:5], tl[:, 3:4], ALU.add))
            step(v.scalar_tensor_tensor(vals[:, 1:2], tl[:, 4:5], -float(P), tl[:, 0:1], ALU.mult, ALU.add))
            step(v.tensor_copy(vals[:, 0:1], tile_p[:, 0:1]))
            step(v.tensor_copy(vals[:, 2:3], tl[:, 1:2]))
            step(v.tensor_scalar(first[:, :], chunk_iota[:, :], tl[:, 4:5], None, ALU.is_equal))
            own()
            step(v.tensor_tensor(tl[:, 6:7], tl[:, 5:6], tile_p[:, 2:3], ALU.is_gt))
            step(v.tensor_scalar(belong[:, :], chunk_iota[:, :], tl[:, 5:6], None, ALU.is_lt))
            own()
            v.scalar_tensor_tensor(belong[:, :], chunk_iota[:, :], tl[:, 4:5], belong[:, :],
                                   ALU.is_ge, ALU.mult).then_inc(s_chunks, 1)
            norm_scales(1)
            norm_stats(2)
            v.wait_ge(s_pe, 3)
            step(v.tensor_copy(info[:, :, :], pA[:, 0:3 * BLOCKS].rearrange("p (j c) -> p j c", c=3)))
            step(v.tensor_scalar(flags[0:1, 1:2], pA[0:1, 32:33], 0.0, None, ALU.is_gt))
            step(v.tensor_copy(flagf[0:1, 0:2], pA[0:1, 34:36]))
            own()
            step(v.tensor_tensor(flagf[0:1, 2:3], flagf[0:1, 0:1], flagf[0:1, 1:2], ALU.add))
            step(v.tensor_tensor(info[:, :, 1], info[:, :, 1], chunk_start[:, :], ALU.add))
            own()
            v.tensor_scalar(flags[0:1, 0:1], flagf[0:1, 2:3], 0.0, None, ALU.is_gt).then_inc(s_dv, 1)
            dv += 1
            step(v.tensor_tensor(info[:, :, 2], info[:, :, 2], info[:, :, 1], ALU.subtract))
            step(v.tensor_scalar(run_start[:, :], info[:, :, 1], float(E), None, ALU.min))
            own()
            v.nop().then_inc(s_flags, 1)
            for q in range(3, STEPS):
                norm_stats(q)
                norm_scales(q - 1)
            norm_scales(STEPS - 1)
            v.wait_ge(s_pe, 4)
            for h in range(2):
                step(v.tensor_scalar(toff[0:1, h * CROW:(h + 1) * CROW], (pB, pC)[h][0:1, 0:CROW],
                                     float(TILES * W), None, ALU.add))
                step(v.tensor_scalar(keep[:, h * CROW:(h + 1) * CROW], (ps[0], ps[1])[h][:, 0:CROW], -1.0, 1.0,
                                     ALU.mult, ALU.add))
            v.wait_ge(s_dv, dv)
            unsorted = v.value_load(flags[0:1, 0:1], min_val=0, max_val=1)
            late = v.value_load(flags[0:1, 1:2], min_val=0, max_val=1)
            with v.If(unsorted > 0):
                v.memset(pos_f[:, :], 0.0).then_inc(s_scan, 1)
                v.tensor_tensor(ncnt[:, :], cntb[:, 1:TILES + 1], cntb[:, 0:TILES], ALU.subtract)\
                    .then_inc(s_scan, 1)
                v.tensor_scalar(diag[:, :], ident[0:TILES, 0:TILES], tl[:, 4:5], float(P), ALU.mult, ALU.mult)\
                    .then_inc(s_scan, 1)
                v.wait_ge(s_scan_pe, 1)
                v.tensor_scalar(slot0[:, :], pA[0:EP, 0:TILES], -1.0, None, ALU.add).then_inc(s_scan, 1)
                v.wait_ge(s_scan, 4)
                with v.Fori(0, TILES) as t:
                    v.tensor_scalar(e_tmp[:, :], e_f[:, :], bound[0:EP, bass.ds(t, 1)], None, ALU.is_ge)\
                        .then_inc(s_scan, 1)
                    v.wait_ge(s_scan, t * 5 + 5)
                    v.scalar_tensor_tensor(e_tmp[:, :], e_f[:, :], bound[0:EP, bass.ds(t + 1, 1)],
                                           e_tmp[:, :], ALU.is_lt, ALU.mult).then_inc(s_scan, 1)
                    v.wait_ge(s_scan, t * 5 + 6)
                    v.tensor_tensor_scan(e_scan[:, :], ones[0:EP, 0:1].to_broadcast([EP, EC]), e_tmp[:, :],
                                         slot0[:, bass.ds(t, 1)], ALU.mult, ALU.add).then_inc(s_scan, 1)
                    v.wait_ge(s_scan, t * 5 + 7)
                    v.tensor_tensor(e_scan[:, :], e_scan[:, :], e_tmp[:, :], ALU.mult).then_inc(s_scan, 1)
                    v.wait_ge(s_scan, t * 5 + 8)
                    v.tensor_tensor(pos_f[:, :], pos_f[:, :], e_scan[:, :], ALU.add).then_inc(s_scan, 1)
                    v.wait_ge(s_scan, t * 5 + 9)
                v.tensor_copy(pos_i[:, :], pos_f[:, :]).then_inc(s_pos, 1)
                v.nop().then_inc(s_posr, 1)
            def turned(n, to, h):
                nonlocal dv
                c = slice(512 * h, min(512 * (h + 1), CP))
                v.wait_ge(s_turn, n)
                v.tensor_copy(to[:, c], ps[n - 1][:, 0:c.stop - c.start]).then_inc(s_dv, 1)
                dv += 1

            v.wait_ge(s_blk, 16)
            step(v.tensor_scalar(u_src[:, :], u_rec, (1 << SRC_BITS) - 1, None, ALU.bitwise_and))
            own()
            v.tensor_copy(u_idx, u_src[:, :]).then_inc(s_unp, 1)
            step(v.tensor_scalar(u_dst[:, :], u_rec, DST_SHIFT, (1 << SRC_BITS) - 1,
                                 ALU.logical_shift_right, ALU.bitwise_and))
            step(v.tensor_scalar(u_rec, u_rec, REL_SHIFT, None, ALU.logical_shift_right))
            turned(1, idx0, 0)
            turned(2, idx0, 1)
            own()
            v.memset(rows[:, :, D:W], 1.0).then_inc(s_sum, GROUP)
            v.nop().then_inc(s_idx0, 1)
            for j in range(BLOCKS):
                step(v.tensor_scalar(u_node[:, j * P:(j + 1) * P], slot_iota[:, :], info[:, j, 2:3], EMPTY,
                                     ALU.is_ge, ALU.mult))
            own()
            for j in range(BLOCKS):
                c = slice(j * P, (j + 1) * P)
                step(v.scalar_tensor_tensor(u_node[:, c], u_dst[:, c], info[:, j, 0:1], u_node[:, c],
                                            ALU.subtract, ALU.add))
            own()
            v.nop().then_inc(s_unp, 1)
            v.scalar_tensor_tensor(u_msg, u_rec, float(N), u_src[:, :], ALU.mult, ALU.add)\
                .then_inc(s_unp, 1)
            turned(3, dloc, 0)
            turned(4, dloc, 1)
            own()
            v.wait_ge(s_sum, GROUP)
            v.nop().then_inc(s_acc0, PS)
            v.nop().then_inc(s_acc, PS)

            def batch_norms():
                third = [slice(l * D, (l + 1) * D) for l in range(LAYERS)]

                def inverse(c):
                    step(v.reciprocal(bn[:, 0, c], bn[:, 0, c]))

                def scales():
                    own()
                    step(v.tensor_tensor(bn[:, 1, :], bn[:, 1, :], bn[:, 0, :], ALU.mult))

                def bias(other, op):
                    own()
                    step(v.tensor_tensor(bnrow[0:1, 0, :], bnrow[0:1, 0, :], other, op))

                def scaled(w, k):
                    own()
                    step(v.tensor_tensor(w[:, :, k, :], w[:, :, k, :],
                                         bn[:, 1, :].rearrange("p (l d) -> p l d", d=D), ALU.mult))

                def biases():
                    step(v.tensor_tensor(bihc[:, 0, :], bihc[:, 0, :], bihc[:, 1, :], ALU.add))

                v.wait_ge(s_bnsq, 1)
                return [lambda c=c: inverse(c) for c in third] + [
                    scales,
                    lambda: bias(bnrow[0:1, 1, :], ALU.subtract),
                    lambda: bias(bn[0:1, 1, :], ALU.mult),
                    lambda: bias(bnrow[0:1, 2, :], ALU.add)] + [
                    lambda w=w, k=k: scaled(w, k) for w in (wl, wr) for k in range(KD)] + [biases]

            for L in range(LAYERS + 1):
                def offsets(i):
                    _, offs = nc.values_load_multi_w_load_instructions(
                        toff[0:1, bass.ds(i * GROUP, GROUP)], engines=(mybir.EngineType.DVE,),
                        min_val=0, max_val=TILES * W,
                        skip_runtime_bounds_check_because="the table is made of offsets of tiles")
                    return offs

                def hot(i, h, L=L):
                    v.wait_ge(s_sum, i * GROUP + (L * CHUNKS + (h + 1) * HALF))
                    v.tensor_tensor(
                        onehot[:, h * HALF:(h + 1) * HALF, :],
                        node_iota[:, :].unsqueeze(1).to_broadcast([P, HALF, TN]),
                        dloc[:, bass.ds(i * GROUP + h * HALF, HALF)].unsqueeze(2)
                        .to_broadcast([P, HALF, TN]), ALU.is_equal).then_inc(s_hot, 1)

                def add(i, u, offs, L=L):
                    v.wait_ge(s_sum, i * GROUP + (L * CHUNKS + GROUP + u + 1))
                    for s_part, c0, c1 in ((s_acc0, 0, P), (s_acc, P, W)):
                        v.wait_ge(s_part, i * GROUP + (L * CHUNKS + PS + u))
                        a = acc[0:TN, bass.ds(offs[u] + c0, c1 - c0)]
                        v.scalar_tensor_tensor(a, a, keep[0:TN, bass.ds(i * GROUP + u, 1)],
                                               ps[u % PS][0:TN, c0:c1], ALU.mult, ALU.add)\
                            .then_inc(s_part, 1)

                def group(i, todo=(), at=()):
                    offs = offsets(i)
                    for u in range(GROUP):
                        add(i, u, offs)
                        if u == HOT_AT[0]:
                            hot(i, 1)
                        if u == HOT_AT[1]:
                            hot(i + 1, 0)
                        if u in at:
                            todo[at.index(u)]()

                if L > 0:
                    v.wait_ge(s_hot, L * (2 * GROUPS + 1))
                v.wait_ge(s_sum, L * CHUNKS + GROUP)
                hot(0, 0)
                if L == 0:
                    todo = batch_norms()
                    half = len(todo) // 2
                    group(0, todo[:half], BN_AT)
                    group(1, todo[half:], BN_AT)
                    own()
                    v.nop().then_inc(s_bnready, 1)
                for i in range(2 if L == 0 else 0, LEAD):
                    group(i)
                with v.If(late == 0):
                    def tile(t, at, L=L):
                        v.wait_ge(s_acc0, t * GROUP + (LEAD * GROUP + L * CHUNKS + PS))
                        v.wait_ge(s_acc, t * GROUP + (LEAD * GROUP + L * CHUNKS + PS))
                        group(t + LEAD, dve_stages(v, L, t, S), at)

                    two = 1 if L == LAYERS - 1 else 0
                    with v.Fori(0, TILES - 1 - two) as t:
                        tile(t, DVE_AT[L])
                    if two:
                        tile(TILES - 2, DVE_TWO)
                    v.wait_ge(s_acc0, (L + 1) * CHUNKS - GROUP + PS)
                    v.wait_ge(s_acc, (L + 1) * CHUNKS - GROUP + PS)
                    for stage in dve_stages(v, L, TILES - 1, S):
                        stage()
                    v.wait_ge(s_hot, (L + 1) * (2 * GROUPS + 1) - 2)
                    v.sem_inc(s_hot, 2)
                    v.sem_inc(s_acc0, GROUP)
                    v.sem_inc(s_acc, GROUP)
                with v.If(late > 0):
                    with v.Fori(0, TILES) as t:
                        group(t + LEAD)
                    v.wait_ge(s_acc0, (L + 1) * CHUNKS + PS)
                    v.wait_ge(s_acc, (L + 1) * CHUNKS + PS)
                    with v.Fori(0, TILES) as t:
                        for stage in dve_stages(v, L, t, S):
                            stage()

        @block.tensor
        def _(pe):
            pe.wait_ge(s_counted, 1)
            pe.wait_ge(s_const, N_CONST)
            pe.matmul(pA[0:TILES, 0:1], cntb[:, 0:TILES], ones[0:EP, 0:1], start=True, stop=True)
            pe.matmul(pA[0:TILES, 1:2], cntb[:, 1:TILES + 1], ones[0:EP, 0:1], start=True, stop=True)\
                .then_inc(s_pe, 1)
            pe.wait_ge(s_chunks, 1)
            pe.matmul(pA[0:TILES, 4:5], tri[0:TILES, 0:TILES], tl[:, 3:4], start=True, stop=True)\
                .then_inc(s_pe, 1)
            pe.wait_ge(s_chunks, 2)
            for j in range(BLOCKS):
                pe.matmul(pA[:, 3 * j:3 * j + 3], belong[:, j * P:(j + 1) * P], vals[:, :],
                          start=True, stop=True)
            pe.matmul(pA[:, 32:33], ones[0:TILES, :], tl[:, 6:7], start=True, stop=True)
            pe.matmul(pA[:, 34:36], ones[0:EP, :], bad[:, 0:2], start=True, stop=True).then_inc(s_pe, 1)
            for h in range(2):
                c = slice(h * CROW, (h + 1) * CROW)
                pe.matmul((pB, pC)[h][0:1, 0:CROW], tile_p[:, 1:2], belong[:, c], start=True, stop=True)
                i = pe.matmul(ps[h][:, 0:CROW], ones[0:TILES, :], first[:, c], start=True, stop=True)
            i.then_inc(s_pe, 1)
            pe.wait_ge(s_flags, 1)
            unsorted = pe.value_load(flags[0:1, 0:1], min_val=0, max_val=1)
            late = pe.value_load(flags[0:1, 1:2], min_val=0, max_val=1)
            with pe.If(unsorted > 0):
                pe.wait_ge(s_scan, 3)
                pe.matmul(pA[0:EP, 0:TILES], tri[0:EP, 0:EP], ncnt[:, :], start=True, stop=False)
                pe.matmul(pA[0:EP, 0:TILES], ones[0:TILES, 0:EP], diag[:, :], start=False, stop=True)\
                    .then_inc(s_scan_pe, 1)
            n = 0
            for k, frm in enumerate((u_idx, u_node, u_msg)):
                pe.wait_ge(s_unp, k + 1)
                for h in range(2):
                    c0, c1 = 512 * h, min(512 * (h + 1), CP)
                    for c in range(c0, c1, P):
                        i = pe.transpose((ps + [pA, pB])[n][:, c - c0:c - c0 + P], frm[:, c:c + P],
                                         ident[:, :])
                    i.then_inc(s_turn, 1)
                    n += 1
            for L in range(LAYERS + 1):
                def product(i, u, last=False, L=L):
                    if u % HALF == 0:
                        pe.wait_ge(s_hot, i * 2 + (L * (2 * GROUPS + 1) + u // HALF + 1))
                    if last:
                        pe.wait_ge(s_rows_last[u], 16 * (L + 1))
                    else:
                        pe.wait_ge(s_rows[u], i * 16 + 16 * (L * (GROUPS - 1) + 1))
                    pe.wait_ge(s_acc, i * GROUP + (L * CHUNKS + u + 1))
                    pe.matmul(ps[u % PS][0:TN, 0:W], onehot[:, u, :], rows[:, u, :], start=True, stop=True)\
                        .then_inc(s_sum, 1)

                with pe.Fori(0, LEAD) as i:
                    for u in range(GROUP):
                        product(i, u)
                if L == 0:
                    pe.wait_ge(s_bnready, 1)
                    pe.wait_ge(s_idx1, 2)
                def group(i, todo, at):
                    for u in range(GROUP):
                        product(i, u)
                        if u in at:
                            todo[at.index(u)]()

                with pe.If(late == 0):
                    if L == LAYERS - 1:
                        group(LEAD, pe_stages(pe, L, 0, S), PE_AT[L][2:4])
                        def both(t):
                            rows_of, msgs_of = pe_stages(pe, L, t + 1, S), pe_messages(pe, t, S)
                            return msgs_of[0:2] + rows_of + msgs_of[2:3]

                        with pe.Fori(0, TILES - 3) as t:
                            group(t + (LEAD + 1), both(t), PE_AT[L])
                        before = pe_messages(pe, TILES - 2, S)
                        group(GROUPS - 2, both(TILES - 3) + before[0:2], PE_TWO)
                        behind = pe_stages(pe, L, TILES - 1, S) + before[2:3] + pe_messages(pe, TILES - 1, S)
                    else:
                        with pe.Fori(0, TILES - 1) as t:
                            group(t + LEAD, pe_stages(pe, L, t, S), PE_AT[L])
                        behind = pe_stages(pe, L, TILES - 1, S)
                    for stage in behind:
                        stage()
                    pe.sem_inc(s_sum, GROUP)
                with pe.If(late > 0):
                    with pe.Fori(0, TILES - 1) as t:
                        group(t + LEAD, (), ())
                    for u in range(GROUP):
                        product(GROUPS - 1, u, last=True)
                    with pe.Fori(0, TILES) as t:
                        for stage in pe_stages(pe, L, t, S) + (pe_messages(pe, t, S) if L == LAYERS - 1 else []):
                            stage()


_NAMES = ["x", "src", "dst", "edge_type_2", "L0_gnn_mask_embed", "L0_gnn_Wl", "L0_gnn_Wr", "L0_gnn_b",
          "L0_gnn_gamma", "L0_gnn_beta", "L0_gnn_rmean", "L0_gnn_rvar", "L1_gnn_W_rel", "L1_gnn_b_rel",
          "L1_gnn_W_ih", "L1_gnn_b_ih", "L1_gnn_b_hh", "L1_gnn_W1", "L1_gnn_b1", "L1_gnn_W2", "L1_gnn_b2",
          "L1_gnn_W3", "L1_gnn_b3"]
_TURNED = ("L1_gnn_W_rel", "L1_gnn_W_ih", "L1_gnn_W1", "L1_gnn_W2", "L1_gnn_W3")


def kernel(**inputs):
    import numpy as _np
    import concourse.bacc as _bacc
    from concourse import mybir as _mybir
    from concourse.bass_utils import run_bass_kernel_spmd as _run

    nc = _bacc.Bacc("TRN2", target_bir_lowering=False, num_devices=1)
    arrays, args = {}, []
    for name in _NAMES:
        a = _np.asarray(inputs[name])
        if name in _TURNED:
            a = _np.swapaxes(a, -1, -2)
        a = _np.ascontiguousarray(a)
        arrays[f"in_{name}_dram"] = a
        args.append(nc.dram_tensor(f"in_{name}_dram", a.shape, _mybir.dt.from_np(a.dtype),
                                   kind="ExternalInput").ap())
    args.append(nc.dram_tensor("out_0_dram", (N, D), _mybir.dt.float32, kind="ExternalOutput").ap())
    gnn(nc, *args)
    r = _run(nc, [arrays], core_ids=[0])
    return r.results[0]["out_0_dram"]
```
